# Optimizing a Trainium2 kernel written in Bass

```python
import numpy as np
import jax
import jax.numpy as jnp

def _softmax(x, axis=-1):
    return jax.nn.softmax(x, axis=axis)

def _gelu(x):
    return jax.nn.gelu(x, approximate=True)

def _silu(x):
    return jax.nn.silu(x)

def _sigmoid(x):
    return jax.nn.sigmoid(x)

def _layernorm(x, axis=-1, eps=1e-05):
    m = jnp.mean(x, axis=axis, keepdims=True)
    v = jnp.var(x, axis=axis, keepdims=True)
    return (x - m) / jnp.sqrt(v + eps)

def _scatter_add(tgt, idx, src, axis=0):
    return tgt.at[idx].add(src)

def _segment_sum(src, seg, n):
    return jax.ops.segment_sum(src, seg, n)
kernel_name = 'mk_conv_attn_hybrid_d2_conv_nchw128_r2_a4537f'

def setup_inputs(seed: int=0):
    np.random.seed(seed)
    _w = jnp.asarray

    def _rec_inputs():
        import jax
        import jax.numpy as jnp
        _gk = jax.random.key(seed)
        x = -0.0005207 + 1.001 * jax.random.normal(jax.random.fold_in(_gk, 1), (4, 64, 32, 32), jnp.float32)
        return x
    x = _rec_inputs()

    def _L0_conv_setup():
        import jax, jax.numpy as jnp
        import numpy as np
        B, C, H, W = (4, 64, 32, 32)
        HEADS = 4
        HD = C // HEADS
        HIDDEN = 2 * C
        EPS = 1e-05

        def layernorm(x, w, b):
            mu = jnp.mean(x, axis=-1, keepdims=True)
            var = jnp.mean(jnp.square(x - mu), axis=-1, keepdims=True)
            return (x - mu) * jax.lax.rsqrt(var + EPS) * w + b
        key = jax.random.key(seed)
        ks = jax.random.split(key, 8)
        s = 0.02
        return {'x': jax.random.normal(ks[0], (B, C, H, W), dtype=jnp.float32), 'ln1_w': jnp.ones((C,), jnp.float32), 'ln1_b': jnp.zeros((C,), jnp.float32), 'qkv_w': jax.random.normal(ks[1], (3 * C, C), jnp.float32) * s, 'proj_w': jax.random.normal(ks[2], (C, C), jnp.float32) * s, 'proj_b': jnp.zeros((C,), jnp.float32), 'ln2_w': jnp.ones((C,), jnp.float32), 'ln2_b': jnp.zeros((C,), jnp.float32), 'fc1_w': jax.random.normal(ks[3], (HIDDEN, C), jnp.float32) * s, 'fc1_b': jnp.zeros((HIDDEN,), jnp.float32), 'fc2_w': jax.random.normal(ks[4], (C, HIDDEN), jnp.float32) * s, 'fc2_b': jnp.zeros((C,), jnp.float32)}
    _L0_conv_all = _L0_conv_setup()
    _L0_conv_in = {k: v for k, v in _L0_conv_all.items() if k in ('ln1_w', 'ln1_b', 'qkv_w', 'proj_w', 'proj_b', 'ln2_w', 'ln2_b', 'fc1_w', 'fc1_b', 'fc2_w', 'fc2_b')}
    del _L0_conv_all

    def _L1_attn_setup():
        import jax, jax.numpy as jnp
        import numpy as np
        EMB, HEADS, K = (64, 8, 32)
        key = jax.random.key(seed)
        ks = jax.random.split(key, 6)
        b, t, e, h = (2, 1024, EMB, HEADS)
        s = 1.0 / np.sqrt(e).astype(np.float32)
        x = jax.random.normal(ks[0], (b, t, e), jnp.float32)
        Wq = jax.random.normal(ks[1], (e * h, e), jnp.float32) * s
        Wk = jax.random.normal(ks[2], (e * h, e), jnp.float32) * s
        Wv = jax.random.normal(ks[3], (e * h, e), jnp.float32) * s
        Wu = jax.random.normal(ks[4], (e, h * e), jnp.float32) * (1.0 / np.sqrt(h * e).astype(np.float32))
        bu = jnp.zeros((e,), jnp.float32)
        return {'x': x, 'Wq': Wq, 'Wk': Wk, 'Wv': Wv, 'Wu': Wu, 'bu': bu}
    _L1_attn_all = _L1_attn_setup()
    _L1_attn_in = {k: v for k, v in _L1_attn_all.items() if k in ('Wq', 'Wk', 'Wv', 'Wu', 'bu')}
    del _L1_attn_all

    def _L1_ffn_setup():
        import jax, jax.numpy as jnp
        import numpy as np
        BN_EPS = 1e-05
        key = jax.random.key(seed)
        k1, k2, k3 = jax.random.split(key, 3)
        B, T, I, H = (32, 1024, 64, 64)
        x = jax.random.normal(k1, (B, T, I), dtype=jnp.float32)
        W = jax.random.normal(k2, (H, I), dtype=jnp.float32) * (1.0 / np.sqrt(I))
        V = jnp.linalg.qr(jax.random.normal(k3, (H, H), dtype=jnp.float32))[0]
        gamma = jnp.ones((H,), dtype=jnp.float32)
        beta = jnp.zeros((H,), dtype=jnp.float32)
        return {'x': x, 'W': W, 'V': V, 'gamma': gamma, 'beta': beta}
    _L1_ffn_all = _L1_ffn_setup()
    _L1_ffn_in = {k: v for k, v in _L1_ffn_all.items() if k in ('W', 'V', 'gamma', 'beta')}
    del _L1_ffn_all
    return {'x': x, 'L0_conv_ln1_w': _L0_conv_in['ln1_w'], 'L0_conv_ln1_b': _L0_conv_in['ln1_b'], 'L0_conv_qkv_w': _L0_conv_in['qkv_w'], 'L0_conv_proj_w': _L0_conv_in['proj_w'], 'L0_conv_proj_b': _L0_conv_in['proj_b'], 'L0_conv_ln2_w': _L0_conv_in['ln2_w'], 'L0_conv_ln2_b': _L0_conv_in['ln2_b'], 'L0_conv_fc1_w': _L0_conv_in['fc1_w'], 'L0_conv_fc1_b': _L0_conv_in['fc1_b'], 'L0_conv_fc2_w': _L0_conv_in['fc2_w'], 'L0_conv_fc2_b': _L0_conv_in['fc2_b'], 'L1_attn_Wq': _L1_attn_in['Wq'], 'L1_attn_Wk': _L1_attn_in['Wk'], 'L1_attn_Wv': _L1_attn_in['Wv'], 'L1_attn_Wu': _L1_attn_in['Wu'], 'L1_attn_bu': _L1_attn_in['bu'], 'L1_ffn_W': _L1_ffn_in['W'], 'L1_ffn_V': _L1_ffn_in['V'], 'L1_ffn_gamma': _L1_ffn_in['gamma'], 'L1_ffn_beta': _L1_ffn_in['beta']}

def reference(x, L0_conv_ln1_w, L0_conv_ln1_b, L0_conv_qkv_w, L0_conv_proj_w, L0_conv_proj_b, L0_conv_ln2_w, L0_conv_ln2_b, L0_conv_fc1_w, L0_conv_fc1_b, L0_conv_fc2_w, L0_conv_fc2_b, L1_attn_Wq, L1_attn_Wk, L1_attn_Wv, L1_attn_Wu, L1_attn_bu, L1_ffn_W, L1_ffn_V, L1_ffn_gamma, L1_ffn_beta):
    import jax
    import jax.numpy as jnp

    def _L0_conv_ref(x, ln1_w, ln1_b, qkv_w, proj_w, proj_b, ln2_w, ln2_b, fc1_w, fc1_b, fc2_w, fc2_b):
        import jax, jax.numpy as jnp
        import numpy as np
        B, C, H, W = (4, 64, 32, 32)
        HEADS = 4
        HD = C // HEADS
        HIDDEN = 2 * C
        EPS = 1e-05

        def layernorm(x, w, b):
            mu = jnp.mean(x, axis=-1, keepdims=True)
            var = jnp.mean(jnp.square(x - mu), axis=-1, keepdims=True)
            return (x - mu) * jax.lax.rsqrt(var + EPS) * w + b
        b, c, h, w = x.shape
        n = h * w
        x_ln = layernorm(jnp.transpose(x, (0, 2, 3, 1)), ln1_w, ln1_b)
        qkv = jnp.einsum('bhwc,oc->bohw', x_ln, qkv_w)
        q, k, v = jnp.split(qkv, 3, axis=1)
        q = q.reshape(b, HEADS, HD, n)
        k = k.reshape(b, HEADS, HD, n)
        v = v.reshape(b, HEADS, HD, n)
        scale = 1.0 / jnp.sqrt(jnp.float32(HD))
        scores = jnp.einsum('bhdn,bhdm->bhnm', q, k) * scale
        attn = jax.nn.softmax(scores, axis=-1)
        out = jnp.einsum('bhnm,bhdm->bhdn', attn, v)
        out = out.reshape(b, c, h, w)
        out = jnp.einsum('bchw,oc->bohw', out, proj_w) + proj_b[None, :, None, None]
        x = x + out
        x_ln2 = layernorm(jnp.transpose(x, (0, 2, 3, 1)), ln2_w, ln2_b)
        x_flat = x_ln2.reshape(b, n, c)
        hdn = jax.nn.gelu(jnp.einsum('bnc,oc->bno', x_flat, fc1_w) + fc1_b, approximate=False)
        x_mlp = jnp.einsum('bno,co->bnc', hdn, fc2_w) + fc2_b
        x_mlp = jnp.transpose(x_mlp.reshape(b, h, w, c), (0, 3, 1, 2))
        return x + x_mlp

    def _L1_attn_ref(x, Wq, Wk, Wv, Wu, bu):
        import jax, jax.numpy as jnp
        import numpy as np
        EMB, HEADS, K = (64, 8, 32)
        b, t, e = x.shape
        h, k = (HEADS, K)
        tp = t + k - 1
        scale = e ** 0.25
        xp = jnp.pad(x, ((0, 0), (k - 1, 0), (0, 0)))
        q = (x @ Wq.T).reshape(b, t, h, e) / scale
        kk = (xp @ Wk.T).reshape(b, tp, h, e) / scale
        v = (xp @ Wv.T).reshape(b, tp, h, e)
        idx = jnp.arange(t)[:, None] + jnp.arange(k)[None, :]
        kw = kk[:, idx]
        vw = v[:, idx]
        dot = jnp.einsum('bthe,btkhe->bthk', q, kw)
        attn = jax.nn.softmax(dot, axis=-1)
        out = jnp.einsum('bthk,btkhe->bthe', attn, vw)
        out = out.reshape(b, t, h * e)
        return out @ Wu.T + bu

    def _L1_ffn_ref(x, W, V, gamma, beta):
        import jax, jax.numpy as jnp
        import numpy as np
        BN_EPS = 1e-05
        B, T, H = (x.shape[0], x.shape[1], W.shape[0])
        Wx = jnp.einsum('bti,hi->bth', x, W)
        flat = Wx.reshape(B * T, H)
        mean = jnp.mean(flat, axis=0)
        var = jnp.var(flat, axis=0)
        Wx = ((flat - mean) * jax.lax.rsqrt(var + BN_EPS) * gamma + beta).reshape(B, T, H)
        Vt = V.T

        def step(yt, wx_t):
            yt = jax.nn.sigmoid(wx_t + yt @ Vt)
            return (yt, yt)
        y0 = jnp.zeros((B, H), dtype=Wx.dtype)
        _, ys = jax.lax.scan(step, y0, jnp.swapaxes(Wx, 0, 1))
        return jnp.swapaxes(ys, 0, 1)

    def _gn(v, G=32, eps=1e-05):
        B_, C_, H_, W_ = v.shape
        g = v.reshape(B_, G, C_ // G, H_, W_)
        m = jnp.mean(g, axis=(2, 3, 4), keepdims=True)
        s = jnp.var(g, axis=(2, 3, 4), keepdims=True)
        return ((g - m) / jnp.sqrt(s + eps)).reshape(v.shape)

    def _ln_c(v, eps=1e-06):
        m = jnp.mean(v, axis=1, keepdims=True)
        s = jnp.var(v, axis=1, keepdims=True)
        return (v - m) / jnp.sqrt(s + eps)

    def _ln_t(v, eps=1e-05):
        m = jnp.mean(v, axis=-1, keepdims=True)
        s = jnp.var(v, axis=-1, keepdims=True)
        return (v - m) / jnp.sqrt(s + eps)

    def _to_tokens(v):
        B_, C_, H_, W_ = v.shape
        return v.reshape(B_, C_, H_ * W_).transpose(0, 2, 1)

    def _from_tokens(t, like):
        B_, C_, H_, W_ = like.shape
        return t.transpose(0, 2, 1).reshape(B_, C_, H_, W_)
    x = _L0_conv_ref(x, L0_conv_ln1_w, L0_conv_ln1_b, L0_conv_qkv_w, L0_conv_proj_w, L0_conv_proj_b, L0_conv_ln2_w, L0_conv_ln2_b, L0_conv_fc1_w, L0_conv_fc1_b, L0_conv_fc2_w, L0_conv_fc2_b)
    t = _to_tokens(x)
    t = t + _L1_attn_ref(_ln_t(t), L1_attn_Wq, L1_attn_Wk, L1_attn_Wv, L1_attn_Wu, L1_attn_bu)
    t = t + _L1_ffn_ref(_ln_t(t), L1_ffn_W, L1_ffn_V, L1_ffn_gamma, L1_ffn_beta)
    x = _from_tokens(t, x)
    return x

_drawn_inputs = setup_inputs


def setup_inputs(seed=0):
    import zlib

    import numpy as np

    out = dict(_drawn_inputs(seed))
    spreads = {'L0_conv_ln1_w': (1.0, 0.6),
     'L0_conv_ln1_b': (0.0, 0.8),
     'L0_conv_proj_b': (0.0, 0.1),
     'L0_conv_ln2_w': (1.0, 0.6),
     'L0_conv_ln2_b': (0.0, 2.0),
     'L0_conv_fc1_b': (0.0, 0.57),
     'L0_conv_fc2_b': (0.0, 0.1),
     'L1_attn_bu': (0.0, 0.1),
     'L1_ffn_gamma': (1.0, 0.6),
     'L1_ffn_beta': (0.0, 0.507)}
    factors = {'L0_conv_qkv_w': 8.0, 'L0_conv_proj_w': 8.0, 'L0_conv_fc1_w': 3.204}
    for name, (base, spread) in spreads.items():
        noise = np.random.default_rng([zlib.crc32(name.encode()), seed]).standard_normal(out[name].shape)
        drawn = base * np.exp(spread * noise) if base else spread * noise
        out[name] = jnp.asarray(drawn.astype(out[name].dtype))
    for name, factor in factors.items():
        out[name] = (out[name] * factor).astype(out[name].dtype)
    return out
```

```python
from contextlib import ExitStack

import concourse.bass as bass
from concourse import mybir

F32 = mybir.dt.float32
BF16 = mybir.dt.bfloat16
I32 = mybir.dt.int32
ALU = mybir.AluOpType
ACT = mybir.ActivationFunctionType
AX_X = mybir.AxisListType.X

P = 128
B, C, N = 4, 64, 1024
HALF = N // 2
H0 = 4
HD = C // H0
HP = P // H0
KT = N // P
PARTS = 3
QTERM = (0, 0, 0, 1, 1, 2)
KTERM = (0, 1, 2, 0, 1, 0)
TERMS = len(QTERM)
KQ = TERMS * HD
MAX_PIECES = H0 * KT * 2
UNITS = KT * 2
MAX_PER_UNIT = MAX_PIECES // UNITS

H1 = 8
W = 32
TQ = 4
TG = HALF // TQ
NG = P // (H1 * TQ)
GU = TG // NG
GK = W + TQ
BLOCKS = HALF // W
BK = 2 * W
BQ = H1 * W
PAD = W - 1
XW = HALF + W
STAGES = 4
BPS = BLOCKS // STAGES
UPS = GU // STAGES
GSEL = 2
UPG = GU // GSEL

L = 16
CH = HALF // L
COLS = B * CH
WARM = 12
ALL_PASSES = 2 * CH
START_TOL = 2.0 ** -22
GRAM_LIMIT = 4.0

CONSTS = ["ident", "mean_c", "mean_all", "shift_half", "den_select", "window_mask", "block_mask",
          "unit_select", "block_ones", "part_scale"]
WEIGHTS = ["wq", "wk", "wv", "wproj", "wfc1", "wfc2", "w1q", "w1k", "w1v", "w1u", "w_in", "v_rec"]
VECTORS = ["ln1_w", "ln1_b", "proj_b", "ln2_w", "ln2_b", "fc1_b", "fc2_b", "attn_b", "gamma", "beta"]


def build(nc, a, out):
    with ExitStack() as ctx:
        def sb(name, shape, dt=F32):
            return ctx.enter_context(nc.sbuf_tensor(name, shape, dt))

        def sem(name):
            return ctx.enter_context(nc.semaphore(name))

        shape_of = {n: list(a[n].shape) for n in CONSTS + WEIGHTS}
        early = {"w1q", "w1k", "w1v", "w1u", "unit_select"}
        t = {n: sb("s_" + n, shape_of[n]) for n in CONSTS + WEIGHTS if n not in early}
        vec = sb("vec", [P, len(VECTORS)])
        v = {n: vec[:, i:i + 1] for i, n in enumerate(VECTORS)}
        eps = sb("eps", [P, 1])
        unit_sel = sb("unit_sel", [PARTS * 2 * UPG, UPG, P], BF16)
        abd = sb("abd", [P, H1, P])
        gbd = sb("gbd", [P, H1, P])

        X = sb("X", [P, B, HALF])
        ln_d = sb("ln_d", [P, HALF])
        ln_q = sb("ln_q", [P, HALF])
        ln_l = sb("ln_l", [P, HALF])
        ln_r = sb("ln_r", [P, HALF])
        ln_y = sb("ln_y", [P, HALF])
        x_ln = sb("x_ln", [P, HALF])
        qk_part = sb("qk_part", [P, PARTS, 2, HALF], BF16)
        qk_rest = sb("qk_rest", [P, 2, HALF])
        QX = [sb(f"QX{i}", [KQ + PARTS, H0, N], BF16) for i in range(2)]
        KX = [sb(f"KX{i}", [KQ + PARTS, H0, N], BF16) for i in range(2)]
        VT = [sb(f"VT{i}", [P, KT, H0, HP]) for i in range(2)]
        part_max = sb("part_max", [P, H0 * KT, 2])
        neg_max = sb("neg_max", [P, PARTS, H0 * KT])
        mx_hi = sb("mx_hi", [P, P], BF16)
        mx_rest = sb("mx_rest", [P, P])
        mx_mid = sb("mx_mid", [P, P], BF16)
        mx_part = sb("mx_part", [P, P], BF16)
        probs = sb("probs", [P, 2, H0, HALF])
        o_sb = sb("o_sb", [P, 2, HALF])
        rden = sb("rden", [P, 2, HALF])
        o_norm = sb("o_norm", [P, 2, HALF])
        x1 = sb("x1", [P, HALF])
        hid = o_norm
        x2 = sb("x2", [P, HALF])

        xh = sb("xh", [P, HALF])
        xbd = sb("xbd", [P, XW, 2])
        xbd16 = sb("xbd16", [P, 2, XW], BF16)
        z = sb("z", [P, TG, H1, TQ])
        zs = sb("zs", [P, GU * 2 * GK + TG * H1 * TQ // 2])
        z16 = zs[:, 0:TG * H1 * TQ // 2].bitcast(BF16).rearrange("p (t h q) -> p t h q", h=H1, q=TQ)
        s_win = zs[:, TG * H1 * TQ // 2:].rearrange("p (s k) -> p s k", k=GK)
        y1 = zs[:, 0:H1 * TG * TQ].rearrange("p (h t q) -> p h t q", h=H1, q=TQ)
        x_tok = sb("x_tok", [P, BLOCKS, P])
        neg_m1 = sb("neg_m1", [P, GSEL, PARTS, 2 * UPG])
        m1_hi = sb("m1_hi", [PARTS * 2 * UPG, GSEL, P], BF16)
        m1_rest = sb("m1_rest", [PARTS * 2 * UPG, GSEL, P])
        m1_mid = sb("m1_mid", [PARTS * 2 * UPG, GSEL, P], BF16)
        m1_part = sb("m1_part", [PARTS * 2 * UPG, GSEL, P], BF16)
        p1 = sb("p1", [P, 2, BPS * BQ])
        rden1 = rden[:, :, :].rearrange("p a n -> p (a n)")
        x3 = sb("x3", [P, B, HALF])
        y1_flat = zs[:, 0:H1 * TG * TQ]
        for i, n in enumerate(("w1q", "w1k", "w1v", "w1u")):
            t[n] = y1_flat[:, i * H1 * C:(i + 1) * H1 * C].rearrange("p (h m) -> p h m", h=H1)
        t["unit_select"] = x_tok[0:PARTS * 2 * UPG, 0:UPG, :]

        wx = sb("wx", [P, L, B, CH])
        ys = probs[:, 0, :, :].rearrange("p a n -> p (a n)").rearrange("p (s b c) -> p s b c", s=L, b=B)
        y0 = sb("y0", [P, B, CH])
        y0n = sb("y0n", [P, B, CH])
        ydiff = sb("ydiff", [P, B, CH])
        stat = sb("stat", [P, 16])
        flag = sb("flag", [1, 2], I32)
        res = probs[:, 1, :, :]

        S = ctx.enter_context(nc.psum_tensor("S", [P, 4, 512], F32))
        O = ctx.enter_context(nc.psum_tensor("O", [P, 2, 512], F32))
        M = ctx.enter_context(nc.psum_tensor("M", [P, 2, 512], F32))

        scratch = nc.dram_tensor("qk_scratch", [B, PARTS, 2, H0, HD, N], BF16, kind="Internal").ap()

        names = """consts_in x_in weights_in fills gel_fill ones_rows abd_mm abd_done gbd_mm unit_sel_done
            ln_mean ln_ctr ln_sq ln_var ln_log ln_rstd ln_norm ln_out
            qk_mm v_mm qk_hi qk_rst qk_mid qk_lo qk_dram qk_in v_copied
            max_mm max_red negmax negmax_t mx_h mx_r mx_m mx_done shift_in
            st_mm exp_done pv_mm o_copied den_mm rden_done o_normed proj_mm x1_done
            fc1_mm gelu_done fc2_mm x2_done
            shift_mm xbd_a xbd_b xbd_pad xbd_cast z_mm z_copied z_cast tok_mm tok_copied
            sw_mm sw_masked sw_max m1_rep m1_t m1_h m1_r m1_m m1_done
            s1_mm p1_exp p1_masked pv1_mm den1_mm rden1_done y1_done fin_mm x3_done
            wx_mm wx_copied wsum mean_mm mean_done sqsum sqs var_mm bn_log bn_rstd bn_a bn_b bn_done
            gram_mm gram_sum gram_share ydiff_m pre_mm y_done ends_mm y0_moved y0_done ydiff_a ydiff_b dmax_t flag_a flag_b flag_read
            xpre_mm xy_done xends_mm xy0_done res_done out_done""".split()
        g = {n: sem(n) for n in names}

        def half_rows(h):
            return slice(h * C, (h + 1) * C)

        lns = []
        for b in range(-2, B):
            if b >= 0:
                lns += [(b, 2), (b, 3), (b, 4)]
            if b + 2 < B:
                lns.append((b + 2, 1))

        def ln_no(b, which):
            return lns.index((b, which))

        def ln_in(b, which):
            return {1: X[:, b, :], 2: x1[:, :], 3: x2[:, :], 4: x3[:, b, :]}[which]

        block = ctx.enter_context(nc.Block())

        @block.sync
        def _(sp):
            for half in range(2):
                sp.dma_start(X[half_rows(half), :, :],
                             a["x"][:, :, half * HALF:(half + 1) * HALF].rearrange("b c n -> c b n")).then_inc(g["x_in"], 16)
            for n in CONSTS:
                src = a[n]
                sp.dma_start(t[n][:] if n not in early else t[n], src).then_inc(g["consts_in"], 16)
            for n in WEIGHTS:
                sp.dma_start(t[n][:] if n not in early else t[n], a[n]).then_inc(g["weights_in"], 16)
            sp.dma_start(vec[:, :], a["vectors"]).then_inc(g["weights_in"], 16)

            def relayout(b):
                sp.wait_ge(g["qk_lo"], b + 1)
                for half in range(2):
                    sp.dma_start(scratch[b].rearrange("p q h d n -> (h d) p q n")[:, :, :, half * HALF:(half + 1) * HALF],
                                 qk_part[half_rows(half), :, :, :]).then_inc(g["qk_dram"], 16)
                sp.wait_ge(g["qk_dram"], 32 * (b + 1))
                if b >= 2:
                    sp.wait_ge(g["st_mm"], 2 * UNITS * (b - 1))
                for r in range(TERMS):
                    for q, (dst, part) in enumerate(((QX[b % 2], QTERM[r]), (KX[b % 2], KTERM[r]))):
                        sp.dma_start(dst[r * HD:(r + 1) * HD, :, :],
                                     scratch[b, part, q].rearrange("h d n -> d h n")).then_inc(g["qk_in"], 16)

            def shift_rows(b):
                sp.wait_ge(g["mx_done"], b + 1)
                for p in range(PARTS):
                    sp.dma_start(QX[b % 2][KQ + p:KQ + p + 1, :, :].rearrange("o h (t n) -> o (h t) n", n=P),
                                 mx_part[p * 32:(p + 1) * 32, :]).then_inc(g["shift_in"], 16)

            relayout(0)
            shift_rows(0)
            relayout(1)
            for b in range(B):
                if b + 1 < B:
                    shift_rows(b + 1)
                if b + 2 < B:
                    relayout(b + 2)
            sp.wait_ge(g["res_done"], 1)
            for half in range(2):
                sp.dma_start(out[:, :, half * HALF:(half + 1) * HALF].rearrange("b c n -> c b n"),
                             res[half_rows(half), :, :]).then_inc(g["out_done"], 16)
            sp.wait_ge(g["out_done"], 32)

        @block.gpsimd
        def _(pool):
            nc.gpsimd.memset(eps[:], 1e-5).then_inc(g["gel_fill"], 1)
            nc.gpsimd.memset(xbd[:], 0.0).then_inc(g["gel_fill"], 1)
            for i in range(2):
                nc.gpsimd.memset(VT[i][:, :, :, 0:HD], 0.0)
                nc.gpsimd.memset(VT[i][:, :, :, HD:HD + 1], 1.0)
                nc.gpsimd.memset(VT[i][:, :, :, HD + 1:], 0.0).then_inc(g["gel_fill"], 1)
            nc.gpsimd.memset(y0[:], 0.0).then_inc(g["gel_fill"], 1)
            pool.wait_ge(g["consts_in"], 16 * len(CONSTS))
            pool.wait_ge(g["gel_fill"], 5)
            nc.gpsimd.tensor_copy(unit_sel[:], t["unit_select"]).then_inc(g["unit_sel_done"], 1)

            def split(b):
                pool.wait_ge(g["qk_rst"], b + 1)
                if b:
                    pool.wait_ge(g["qk_dram"], 32 * b)
                nc.gpsimd.tensor_copy(qk_part[:, 1], qk_rest[:, :, :]).then_inc(g["qk_mid"], 1)
                pool.wait_ge(g["qk_mid"], b + 1)
                nc.gpsimd.tensor_tensor(qk_part[:, 2], qk_rest[:, :, :], qk_part[:, 1], ALU.subtract).then_inc(g["qk_lo"], 1)

            def keys(b):
                pool.wait_ge(g["ln_norm"], ln_no(b, 3) + 1)
                if b:
                    pool.wait_ge(g["s1_mm"], STAGES * b)
                    pool.wait_ge(g["tok_mm"], STAGES * b)
                nc.gpsimd.tensor_copy(xbd[0:C, PAD:PAD + HALF, 0], xh[0:C, :])
                nc.gpsimd.tensor_copy(xbd[C:P, PAD:PAD + HALF, 1], xh[C:P, :]).then_inc(g["xbd_a"], 1)
                pool.wait_ge(g["xbd_a"], b + 1)
                pool.wait_ge(g["xbd_pad"], b + 1)
                if b:
                    pool.wait_ge(g["sw_mm"], STAGES * b)
                nc.gpsimd.tensor_copy(xbd16[:], xbd[:].rearrange("p k a -> p a k")).then_inc(g["xbd_cast"], 1)

            split(0)
            split(1)
            for b in range(B):
                keys(b)
                if b + 2 < B:
                    split(b + 2)

        @block.tensor
        def _(pe):
            mm = nc.tensor.matmul

            def layernorm(b, which):
                i = ln_no(b, which)
                mm(S[:, 0, :], t["mean_c"][:], ln_in(b, which), start=True, stop=True).then_inc(g["ln_mean"], 1)
                pe.wait_ge(g["ln_sq"], i + 1)
                mm(S[:, 1, :], t["mean_c"][:], ln_q[:], start=True, stop=True).then_inc(g["ln_var"], 1)

            def project(b):
                layernorm(b, 1)
                pe.wait_ge(g["ln_out"], b + 1)
                mm(S[:, 2, :], t["wq"][:], x_ln[:], start=True, stop=True)
                mm(S[:, 3, :], t["wk"][:], x_ln[:], start=True, stop=True).then_inc(g["qk_mm"], 1)
                for j in range(KT // 2):
                    last = mm(S[:, 0, j * P:(j + 1) * P], x_ln[:, j * P:(j + 1) * P], t["wv"][:], start=True, stop=True)
                last.then_inc(g["v_mm"], 1)

            def max_piece(b, i):
                h, rest = divmod(i, KT * 2)
                nt, kh = divmod(rest, 2)
                n = b * MAX_PIECES + i
                if i == 0:
                    pe.wait_ge(g["qk_in"], 16 * 2 * TERMS * (b + 1))
                    if b:
                        pe.wait_ge(g["mx_r"], b)
                        pe.wait_ge(g["y1_done"], STAGES * (b - 1)) if b >= 2 else None
                if n >= 2:
                    pe.wait_ge(g["max_red"], n - 1)
                mm(M[:, n % 2, :], QX[b % 2][0:KQ, h, nt * P:(nt + 1) * P], KX[b % 2][0:KQ, h, kh * 512:(kh + 1) * 512],
                   start=True, stop=True).then_inc(g["max_mm"], 1)

            def max_rows(b):
                pe.wait_ge(g["negmax"], b + 1)
                mm(M[0:PARTS * 32, 0, 0:P], neg_max[:], t["ident"][:], start=True, stop=True).then_inc(g["negmax_t"], 1)

            def scores_t(b, u, pair):
                nh, j = divmod(u, KT)
                n = (b * UNITS + u) * 2 + pair
                if u:
                    pe.wait_ge(g["exp_done"], n - 1)
                for k in range(2):
                    h = pair * 2 + k
                    last = mm(S[:, h, :], KX[b % 2][:, h, j * P:(j + 1) * P], QX[b % 2][:, h, nh * 512:(nh + 1) * 512],
                              start=True, stop=True)
                last.then_inc(g["st_mm"], 1)

            def values(b, u):
                nh, j = divmod(u, KT)
                n = b * UNITS + u
                pe.wait_ge(g["exp_done"], 2 * (n + 1))
                for h in range(H0):
                    last = mm(O[h * HP:(h + 1) * HP, nh, :], VT[b % 2][:, j, h, :], probs[:, u % 2, h, :],
                              start=(j == 0), stop=(j == KT - 1))
                last.then_inc(g["pv_mm"], 1)

            def attend(b):
                pe.wait_ge(g["shift_in"], 16 * PARTS * (b + 1))
                pe.wait_ge(g["v_copied"], b + 1)
                if b + 1 < B:
                    pe.wait_ge(g["v_copied"], b + 2)
                    pe.wait_ge(g["qk_rst"], b + 2)
                if b:
                    pe.wait_ge(g["wx_copied"], b)
                for pair in range(2):
                    scores_t(b, 0, pair)
                for u in range(UNITS):
                    if u + 1 < UNITS:
                        for pair in range(2):
                            scores_t(b, u + 1, pair)
                    if b + 1 < B:
                        for i in range(MAX_PER_UNIT * u, MAX_PER_UNIT * (u + 1)):
                            max_piece(b + 1, i)
                    values(b, u)
                if b + 1 < B:
                    max_rows(b + 1)

            def finish_first(b):
                pe.wait_ge(g["o_copied"], b + 1)
                for nh in range(2):
                    last = mm(S[:, nh, :], t["den_select"][:], o_sb[:, nh, :], start=True, stop=True)
                last.then_inc(g["den_mm"], 1)
                pe.wait_ge(g["o_normed"], b + 1)
                for nh in range(2):
                    last = mm(S[half_rows(nh), 2, :], t["wproj"][:], o_norm[:, nh, :], start=True, stop=True)
                last.then_inc(g["proj_mm"], 1)
                pe.wait_ge(g["x1_done"], b + 1)
                layernorm(b, 2)
                pe.wait_ge(g["ln_out"], n_out(b, 2))
                for nh in range(2):
                    last = mm(S[:, 2 + nh, :], t["wfc1"][:, nh, :], x_ln[:], start=True, stop=True)
                last.then_inc(g["fc1_mm"], 1)
                pe.wait_ge(g["gelu_done"], b + 1)
                for nh in range(2):
                    last = mm(S[half_rows(nh), 0, :], t["wfc2"][:], hid[:, nh, :], start=True, stop=True)
                last.then_inc(g["fc2_mm"], 1)

            def second(b):
                pe.wait_ge(g["x2_done"], b + 1)
                layernorm(b, 3)
                pe.wait_ge(g["ln_norm"], ln_no(b, 3) + 1)
                mm(S[:, 0, 0:PAD], t["shift_half"][:], xh[:, HALF - PAD:HALF], start=True, stop=True).then_inc(g["shift_mm"], 1)
                zb = ((S, 2), (O, 0))
                for i in range(H1 // 2):
                    n = b * (H1 // 2) + i
                    if i >= 2:
                        pe.wait_ge(g["z_copied"], n - 1)
                    buf, o = zb[i % 2]
                    for k in range(2):
                        last = mm(buf[:, o + k, :], abd[:, 2 * i + k, :], xh[:], start=True, stop=True)
                    last.then_inc(g["z_mm"], 1)
                pe.wait_ge(g["xbd_a"], b + 1)
                pe.wait_ge(g["xbd_pad"], b + 1)
                for r in range(STAGES):
                    n = b * STAGES + r
                    if r >= 2:
                        pe.wait_ge(g["tok_copied"], n - 1)
                    for k in range(BPS):
                        i = r * BPS + k
                        last = mm(S[:, r % 2, k * P:(k + 1) * P], xbd[:, i * W:i * W + BK, :].rearrange("p k a -> p (k a)"), t["ident"][:], start=True, stop=True)
                    last.then_inc(g["tok_mm"], 1)
                pe.wait_ge(g["tok_copied"], (b + 1) * STAGES)
                pe.wait_ge(g["z_copied"], (b + 1) * (H1 // 2))
                pe.wait_ge(g["xbd_cast"], b + 1)
                pe.wait_ge(g["z_cast"], b + 1)
                for r in range(STAGES):
                    n = b * STAGES + r
                    if r >= 2:
                        pe.wait_ge(g["sw_masked"], n - 1)
                    for k in range(UPS):
                        u = r * UPS + k
                        bank, slot = 2 * (r % 2) + k // 4, k % 4
                        for gi in range(NG):
                            tg = u * NG + gi
                            o = slot * 2 * GK
                            last = mm(S[gi * 32:(gi + 1) * 32, bank, o:o + 2 * GK], z16[:, tg, :, :],
                                      xbd16[:, :, tg * TQ:tg * TQ + GK], start=True, stop=True)
                    last.then_inc(g["sw_mm"], 1)
                pe.wait_ge(g["m1_rep"], b + 1)
                for gs in range(GSEL):
                    last = mm(S[0:PARTS * 2 * UPG, 0, gs * P:(gs + 1) * P], neg_m1[:, gs, :, :], t["ident"][:], start=True, stop=True)
                last.then_inc(g["m1_t"], 1)
                pe.wait_ge(g["m1_done"], b + 1)

                def block_scores(r):
                    n = b * STAGES + r
                    if r >= 2:
                        pe.wait_ge(g["p1_exp"], n - 1)
                    for k in range(BPS):
                        i = r * BPS + k
                        bank, o = 2 * (r % 2) + k // 2, (k % 2) * BQ
                        mm(S[:, bank, o:o + BQ], xbd[:, i * W:i * W + BK, :].rearrange("p k a -> p (k a)"), z[:, i * 8:(i + 1) * 8, :, :], start=True, stop=False)
                        for uu in range(2):
                            u = 2 * i + uu
                            last = mm(S[:, bank, o + uu * P:o + (uu + 1) * P], unit_sel[:, u % UPG, :], m1_part[:, u // UPG, :],
                                      start=False, stop=(uu == 1))
                    last.then_inc(g["s1_mm"], 1)

                block_scores(0)
                for r in range(STAGES):
                    n = b * STAGES + r
                    if r + 1 < STAGES:
                        block_scores(r + 1)
                    pe.wait_ge(g["p1_masked"], n + 1)
                    if r:
                        pe.wait_ge(g["y1_done"], n)
                    for k in range(2):
                        last = mm(M[:, k, :], t["block_ones"][:], p1[:, r % 2, k * 512:(k + 1) * 512], start=True, stop=True)
                    last.then_inc(g["den1_mm"], 1)
                    for k in range(BPS):
                        i = r * BPS + k
                        last = mm(O[:, k // 2, (k % 2) * BQ:(k % 2 + 1) * BQ], x_tok[:, i, :], p1[:, r % 2, k * BQ:(k + 1) * BQ],
                                  start=True, stop=True)
                    last.then_inc(g["pv1_mm"], 1)
                pe.wait_ge(g["y1_done"], (b + 1) * STAGES)
                for h in range(H1):
                    last = mm(S[:, 0, :], gbd[:, h, :], y1[:, h, :, :], start=(h == 0), stop=(h == H1 - 1))
                last.then_inc(g["fin_mm"], 1)
                pe.wait_ge(g["x3_done"], b + 1)
                layernorm(b, 4)
                pe.wait_ge(g["ln_norm"], ln_no(b, 4) + 1)
                mm(S[:, 2, :], t["w_in"][:], xh[:], start=True, stop=True).then_inc(g["wx_mm"], 1)
                pe.wait_ge(g["wx_copied"], b + 1)

            def n_out(b, which):
                return outs.index((b, which)) + 1

            outs = [x for x in lns if x[1] in (1, 2)]

            pe.wait_ge(g["x_in"], 32)
            pe.wait_ge(g["consts_in"], 16 * len(CONSTS))
            pe.wait_ge(g["weights_in"], 16 * (len(WEIGHTS) + 1))

            def project_(b):
                layernorm(b, 1)
                pe.wait_ge(g["ln_out"], n_out(b, 1))
                mm(S[:, 2, :], t["wq"][:], x_ln[:], start=True, stop=True)
                mm(S[:, 3, :], t["wk"][:], x_ln[:], start=True, stop=True).then_inc(g["qk_mm"], 1)
                for j in range(KT // 2):
                    last = mm(S[:, 0, j * P:(j + 1) * P], x_ln[:, j * P:(j + 1) * P], t["wv"][:], start=True, stop=True)
                last.then_inc(g["v_mm"], 1)

            for h in range(H1):
                for half in range(2):
                    last = mm(O[half_rows(half), h // 4, (h % 4) * P + half * C:(h % 4) * P + (half + 1) * C],
                              t["w1q"][:, h, :], t["w1k"][:, h, :], start=True, stop=True)
            last.then_inc(g["abd_mm"], 1)
            for h in range(H1):
                for half in range(2):
                    last = mm(M[half_rows(half), h // 4, (h % 4) * P + half * C:(h % 4) * P + (half + 1) * C],
                              t["w1v"][:, h, :], t["w1u"][:, h, :], start=True, stop=True)
            last.then_inc(g["gbd_mm"], 1)
            project_(0)
            pe.wait_ge(g["unit_sel_done"], 1)
            pe.wait_ge(g["ones_rows"], 2)
            pe.wait_ge(g["abd_done"], 4)
            for i in range(MAX_PIECES):
                max_piece(0, i)
            max_rows(0)
            pe.wait_ge(g["v_copied"], 1)
            pe.wait_ge(g["qk_rst"], 1)
            project_(1)
            for b in range(B):
                attend(b)
                finish_first(b)
                second(b)
                if b + 2 < B:
                    project_(b + 2)

            pe.wait_ge(g["wsum"], 1)
            mm(S[:, 0, 0:1], t["mean_all"][:], stat[:, 4:5], start=True, stop=True).then_inc(g["mean_mm"], 1)
            pe.wait_ge(g["sqs"], 1)
            mm(S[:, 1, 0:1], t["mean_all"][:], stat[:, 6:7], start=True, stop=True).then_inc(g["var_mm"], 1)
            pe.wait_ge(g["bn_done"], 1)

            def rnn_step(step, prev, wait_prev, signal):
                bank = M[:, step % 2, 0:COLS]
                mm(bank, t["ident"][:], wx[:, step].rearrange("p b c -> p (b c)"), start=True, stop=False)
                wait_prev()
                mm(bank, t["v_rec"][:], prev.rearrange("p b c -> p (b c)"), start=False, stop=True).then_inc(signal, 1)

            mm(S[:, 2, 0:P], t["v_rec"][:], t["v_rec"][:], start=True, stop=True).then_inc(g["gram_mm"], 1)
            for ps, first in enumerate((L - WARM, 0)):
                for step in range(first, L):
                    n = ps * WARM + step - first

                    def wait_prev(step=step, n=n, first=first, ps=ps):
                        if step > first:
                            pe.wait_ge(g["y_done"], n)
                        elif ps:
                            pe.wait_ge(g["y0_done"], 1)
                    if n >= 2:
                        pe.wait_ge(g["y_done"], n - 1)
                    rnn_step(step, ys[:, step - 1] if step > first else y0[:], wait_prev, g["pre_mm"])
                pe.wait_ge(g["y_done"], n + 1)
                mm(S[:, 0, 0:B], t["shift_half"][:], ys[:, L - 1, :, CH - 1], start=True, stop=True).then_inc(g["ends_mm"], 1)
            pe.wait_ge(g["ydiff_b"], 1)
            mm(S[0:1, 1, 0:P], stat[:, 12:13], t["ident"][:], start=True, stop=True).then_inc(g["dmax_t"], 1)
            pe.wait_ge(g["flag_b"], 1)
            moved = pe.value_load(flag[0:1, 0:1])
            with pe.If(moved):
                with pe.Fori(0, ALL_PASSES) as i:
                    for step in range(L):
                        if step >= 2:
                            pe.wait_ge(g["xy_done"], i * L + step - 1)

                        def wait_prev(step=step):
                            if step:
                                pe.wait_ge(g["xy_done"], i * L + step)
                        rnn_step(step, ys[:, step - 1] if step else y0[:], wait_prev, g["xpre_mm"])
                    pe.wait_ge(g["xy_done"], i * L + L)
                    mm(S[:, 0, 0:B], t["shift_half"][:], ys[:, L - 1, :, CH - 1], start=True, stop=True).then_inc(g["xends_mm"], 1)
                    pe.wait_ge(g["xy0_done"], i + 1)

        @block.scalar
        def _(act):
            A = nc.scalar.activation

            def layernorm(b, which):
                i = ln_no(b, which)
                act.wait_ge(g["ln_ctr"], i + 1)
                A(ln_q[:], ln_d[:], ACT.Square).then_inc(g["ln_sq"], 1)
                act.wait_ge(g["ln_var"], i + 1)
                A(ln_l[:], S[:, 1, :], ACT.Ln, bias=eps[:, 0:1]).then_inc(g["ln_log"], 1)
                act.wait_ge(g["ln_log"], i + 1)
                A(ln_r[:], ln_l[:], ACT.Exp, scale=-0.5).then_inc(g["ln_rstd"], 1)

            def project(b):
                layernorm(b, 1)
                act.wait_ge(g["qk_mm"], b + 1)
                if b:
                    act.wait_ge(g["qk_dram"], 32 * b)
                A(qk_part[:, 0], S[:, 2:4, :], ACT.Copy).then_inc(g["qk_hi"], 1)
                act.wait_ge(g["v_mm"], b + 1)
                if b >= 2:
                    act.wait_ge(g["pv_mm"], UNITS * (b - 1))
                for half in range(2):
                    last = A(VT[b % 2][:, half * 4:half * 4 + 4, :, 0:HD],
                             S[:, 0, :].rearrange("p (j a h d) -> p a j h d", j=4, a=2, h=H0)[:, half], ACT.Copy)
                last.then_inc(g["v_copied"], 1)

            def second(b):
                layernorm(b, 3)
                zb = ((S, 2), (O, 0))
                for i in range(H1 // 2):
                    act.wait_ge(g["z_mm"], b * (H1 // 2) + i + 1)
                    buf, o = zb[i % 2]
                    for k in range(2):
                        last = A(z[:, :, 2 * i + k, :], buf[:, o + k, :].rearrange("p (t q) -> p t q", q=TQ), ACT.Copy)
                    last.then_inc(g["z_copied"], 1)
                for r in range(STAGES):
                    n = b * STAGES + r
                    act.wait_ge(g["s1_mm"], n + 1)
                    if n >= 2:
                        act.wait_ge(g["pv1_mm"], n - 1)
                    A(p1[:, r % 2, :], S[:, 2 * (r % 2):2 * (r % 2) + 2, :], ACT.Exp).then_inc(g["p1_exp"], 1)
                layernorm(b, 4)
                act.wait_ge(g["wx_mm"], b + 1)
                A(wx[:, :, b, :], S[:, 2, :].rearrange("p (c s) -> p s c", s=L), ACT.Copy,
                  accum_out=stat[:, b:b + 1]).then_inc(g["wx_copied"], 1)

            act.wait_ge(g["gel_fill"], 5)
            nc.scalar.preload_act_table_set("natural_log_exp_and_others")
            act.wait_ge(g["abd_mm"], 1)
            act.wait_ge(g["fills"], 2)
            for half in range(2):
                A(abd[half_rows(half), :, half_rows(half)],
                  O[half_rows(half), :, :].rearrange("p k (h m) -> p (k h) m", h=4)[:, :, half_rows(half)],
                  ACT.Copy, scale=0.125).then_inc(g["abd_done"], 1)
            act.wait_ge(g["gbd_mm"], 1)
            for half in range(2):
                A(gbd[half_rows(half), :, half_rows(half)],
                  M[half_rows(half), :, :].rearrange("p k (h m) -> p (k h) m", h=4)[:, :, half_rows(half)],
                  ACT.Copy).then_inc(g["abd_done"], 1)
            project(0)
            project(1)
            for b in range(B):
                for u in range(UNITS):
                    n = b * UNITS + u
                    if n >= 2:
                        act.wait_ge(g["pv_mm"], n - 1)
                    for pair in range(2):
                        act.wait_ge(g["st_mm"], 2 * n + pair + 1)
                        A(probs[:, u % 2, 2 * pair:2 * pair + 2, :], S[:, 2 * pair:2 * pair + 2, :], ACT.Exp,
                          scale=HD ** -0.5).then_inc(g["exp_done"], 1)
                layernorm(b, 2)
                act.wait_ge(g["fc1_mm"], b + 1)
                A(hid[:, :, :], S[:, 2:4, :], ACT.Gelu, bias=v["fc1_b"]).then_inc(g["gelu_done"], 1)
                nc.scalar.preload_act_table_set("natural_log_exp_and_others")
                second(b)
                if b + 2 < B:
                    project(b + 2)
            act.wait_ge(g["mean_done"], 1)
            A(res[:].rearrange("p b n -> p (b n)"), wx[:].rearrange("p s b c -> p (s b c)"), ACT.Square,
              bias=stat[:, 5:6], accum_out=stat[:, 6:7]).then_inc(g["sqs"], 1)
            act.wait_ge(g["var_mm"], 1)
            A(stat[:, 7:8], S[:, 1, 0:1], ACT.Ln, bias=eps[:, 0:1]).then_inc(g["bn_log"], 1)
            act.wait_ge(g["bn_log"], 1)
            A(stat[:, 8:9], stat[:, 7:8], ACT.Exp, scale=-0.5).then_inc(g["bn_rstd"], 1)
            nc.scalar.preload_act_table(ACT.Sigmoid)
            for n, step in enumerate([*range(L - WARM, L), *range(L)]):
                act.wait_ge(g["pre_mm"], n + 1)
                A(ys[:, step].rearrange("p b c -> p (b c)"), M[:, step % 2, 0:COLS], ACT.Sigmoid).then_inc(g["y_done"], 1)
            act.wait_ge(g["flag_b"], 1)
            moved = act.value_load(flag[0:1, 0:1])
            with act.If(moved):
                with act.Fori(0, ALL_PASSES) as i:
                    for step in range(L):
                        act.wait_ge(g["xpre_mm"], i * L + step + 1)
                        A(ys[:, step].rearrange("p b c -> p (b c)"), M[:, step % 2, 0:COLS], ACT.Sigmoid).then_inc(g["xy_done"], 1)

        @block.vector
        def _(dve):
            TT, TS, STT = nc.vector.tensor_tensor, nc.vector.tensor_scalar, nc.vector.scalar_tensor_tensor

            def layernorm(b, which, dst):
                i = ln_no(b, which)
                dve.wait_ge(g["ln_mean"], i + 1)
                TT(ln_d[:], ln_in(b, which), S[:, 0, :], ALU.subtract).then_inc(g["ln_ctr"], 1)
                dve.wait_ge(g["ln_rstd"], i + 1)
                TT(dst, ln_d[:], ln_r[:], ALU.mult).then_inc(g["ln_norm"], 1)

            def affine(b, which, w, bias):
                dve.wait_ge(g["ln_norm"], ln_no(b, which) + 1)
                TS(x_ln[:], ln_y[:], v[w], v[bias], ALU.mult, ALU.add).then_inc(g["ln_out"], 1)

            def project(b):
                layernorm(b, 1, ln_y[:])
                affine(b, 1, "ln1_w", "ln1_b")
                dve.wait_ge(g["qk_hi"], b + 1)
                if b:
                    dve.wait_ge(g["qk_lo"], b)
                TT(qk_rest[:, :, :], S[:, 2:4, :], qk_part[:, 0], ALU.subtract).then_inc(g["qk_rst"], 1)

            def max_piece(b, i):
                h, rest = divmod(i, KT * 2)
                nt, kh = divmod(rest, 2)
                n = b * MAX_PIECES + i
                dve.wait_ge(g["max_mm"], n + 1)
                nc.vector.tensor_reduce(part_max[:, h * KT + nt, kh:kh + 1], M[:, n % 2, :], AX_X, ALU.max).then_inc(g["max_red"], 1)

            def max_rows(b):
                dve.wait_ge(g["max_red"], (b + 1) * MAX_PIECES)
                for p in range(PARTS):
                    last = nc.vector.tensor_reduce(neg_max[:, p, :], part_max[:, :, :], AX_X, ALU.max, negate=True)
                last.then_inc(g["negmax"], 1)
                dve.wait_ge(g["negmax_t"], b + 1)
                if b:
                    dve.wait_ge(g["shift_in"], 16 * PARTS * b)
                r = slice(0, PARTS * 32)
                nc.vector.tensor_copy(mx_hi[r], M[r, 0, 0:P]).then_inc(g["mx_h"], 1)
                dve.wait_ge(g["mx_h"], b + 1)
                STT(mx_rest[r], mx_hi[r], t["part_scale"][r, 0:1], M[r, 0, 0:P], ALU.mult, ALU.add).then_inc(g["mx_r"], 1)
                dve.wait_ge(g["mx_r"], b + 1)
                nc.vector.tensor_copy(mx_mid[r], mx_rest[r]).then_inc(g["mx_m"], 1)
                dve.wait_ge(g["mx_m"], b + 1)
                STT(mx_part[r], mx_mid[r], t["part_scale"][r, 1:2], mx_rest[r], ALU.mult, ALU.add).then_inc(g["mx_done"], 1)

            def finish_first(b):
                dve.wait_ge(g["pv_mm"], UNITS * (b + 1))
                nc.vector.tensor_copy(o_sb[:], O[:]).then_inc(g["o_copied"], 1)
                dve.wait_ge(g["den_mm"], b + 1)
                nc.vector.reciprocal(rden[:], S[:, 0:2, :]).then_inc(g["rden_done"], 1)
                dve.wait_ge(g["rden_done"], b + 1)
                TT(o_norm[:], o_sb[:], rden[:], ALU.mult).then_inc(g["o_normed"], 1)
                dve.wait_ge(g["proj_mm"], b + 1)
                STT(x1[:], S[:, 2, :], v["proj_b"], X[:, b, :], ALU.add, ALU.add).then_inc(g["x1_done"], 1)
                layernorm(b, 2, ln_y[:])
                affine(b, 2, "ln2_w", "ln2_b")
                dve.wait_ge(g["fc2_mm"], b + 1)
                STT(x2[:], S[:, 0, :], v["fc2_b"], x1[:], ALU.add, ALU.add).then_inc(g["x2_done"], 1)

            def second(b):
                layernorm(b, 3, xh[:])
                dve.wait_ge(g["shift_mm"], b + 1)
                nc.vector.tensor_copy(xbd[C:P, 0:PAD, 1], S[C:P, 0, 0:PAD]).then_inc(g["xbd_pad"], 1)
                for r in range(STAGES):
                    dve.wait_ge(g["tok_mm"], b * STAGES + r + 1)
                    nc.vector.tensor_copy(x_tok[:, r * BPS:(r + 1) * BPS, :],
                                          S[:, r % 2, :].rearrange("p (k m) -> p k m", m=P)).then_inc(g["tok_copied"], 1)
                dve.wait_ge(g["z_copied"], (b + 1) * (H1 // 2))
                nc.vector.tensor_copy(z16, z[:]).then_inc(g["z_cast"], 1)
                for r in range(STAGES):
                    dve.wait_ge(g["sw_mm"], b * STAGES + r + 1)
                    for k in range(2):
                        last = TT(s_win[:, (r * UPS + k * 4) * 2:(r * UPS + k * 4 + 4) * 2, :],
                                  S[:, 2 * (r % 2) + k, 0:8 * GK].rearrange("p (s k) -> p s k", k=GK),
                                  t["window_mask"][:].rearrange("p (s k) -> p s k", k=GK), ALU.add)
                    last.then_inc(g["sw_masked"], 1)
                dve.wait_ge(g["sw_masked"], (b + 1) * STAGES)
                nc.vector.tensor_reduce(neg_m1[:, :, 0, :], s_win.rearrange("p (g s) k -> p g s k", g=GSEL), AX_X, ALU.max,
                                        negate=True).then_inc(g["sw_max"], 1)
                dve.wait_ge(g["sw_max"], b + 1)
                nc.vector.tensor_copy(neg_m1[:, :, 1, :], neg_m1[:, :, 0, :])
                nc.vector.tensor_copy(neg_m1[:, :, 2, :], neg_m1[:, :, 0, :]).then_inc(g["m1_rep"], 1)
                dve.wait_ge(g["m1_t"], b + 1)
                r = slice(0, PARTS * 2 * UPG)
                ps = S[r, 0, 0:GSEL * P].rearrange("p (g n) -> p g n", g=GSEL)
                nc.vector.tensor_copy(m1_hi[:], ps).then_inc(g["m1_h"], 1)
                dve.wait_ge(g["m1_h"], b + 1)
                STT(m1_rest[:], m1_hi[:], t["part_scale"][r, 0:1], ps, ALU.mult, ALU.add).then_inc(g["m1_r"], 1)
                dve.wait_ge(g["m1_r"], b + 1)
                nc.vector.tensor_copy(m1_mid[:], m1_rest[:]).then_inc(g["m1_m"], 1)
                dve.wait_ge(g["m1_m"], b + 1)
                STT(m1_part[:], m1_mid[:], t["part_scale"][r, 1:2], m1_rest[:], ALU.mult, ALU.add).then_inc(g["m1_done"], 1)
                def mask(r):
                    n = b * STAGES + r
                    dve.wait_ge(g["p1_exp"], n + 1)
                    blk = p1[:, r % 2, :]
                    TT(blk, blk, t["block_mask"][:], ALU.min).then_inc(g["p1_masked"], 1)

                mask(0)
                for r in range(STAGES):
                    n = b * STAGES + r
                    if r + 1 < STAGES:
                        mask(r + 1)
                    dve.wait_ge(g["den1_mm"], n + 1)
                    nc.vector.reciprocal(rden1[:], M[:]).then_inc(g["rden1_done"], 1)
                    dve.wait_ge(g["pv1_mm"], n + 1)
                    dve.wait_ge(g["rden1_done"], n + 1)
                    for k in range(2):
                        tg = r * (TG // STAGES) + k * (TG // STAGES // 2)
                        last = TT(y1[:, :, tg:tg + TG // STAGES // 2, :].rearrange("p h t q -> p t h q"),
                                  O[:, k, :].rearrange("p (t h q) -> p t h q", h=H1, q=TQ),
                                  rden1[:, k * 512:(k + 1) * 512].rearrange("p (t h q) -> p t h q", h=H1, q=TQ), ALU.mult)
                    last.then_inc(g["y1_done"], 1)
                dve.wait_ge(g["fin_mm"], b + 1)
                STT(x3[:, b, :], S[:, 0, :], v["attn_b"], x2[:], ALU.add, ALU.add).then_inc(g["x3_done"], 1)
                layernorm(b, 4, xh[:])

            for i in range(2):
                nc.vector.memset(KX[i][KQ:KQ + PARTS, :, :], 1.0).then_inc(g["ones_rows"], 1)
            nc.vector.memset(abd[:], 0.0).then_inc(g["fills"], 1)
            nc.vector.memset(gbd[:], 0.0).then_inc(g["fills"], 1)
            dve.wait_ge(g["x_in"], 32)
            dve.wait_ge(g["consts_in"], 16 * len(CONSTS))
            dve.wait_ge(g["weights_in"], 16 * (len(WEIGHTS) + 1))
            project(0)
            for i in range(MAX_PIECES):
                max_piece(0, i)
            max_rows(0)
            project(1)
            for b in range(B):
                if b + 1 < B:
                    for i in range(MAX_PIECES):
                        max_piece(b + 1, i)
                    max_rows(b + 1)
                finish_first(b)
                second(b)
                if b + 2 < B:
                    project(b + 2)

            dve.wait_ge(g["wx_copied"], B)
            nc.vector.tensor_reduce(stat[:, 4:5], stat[:, 0:4], AX_X, ALU.add).then_inc(g["wsum"], 1)
            dve.wait_ge(g["mean_mm"], 1)
            TS(stat[:, 5:6], S[:, 0, 0:1], -1.0, None, ALU.mult).then_inc(g["mean_done"], 1)
            dve.wait_ge(g["bn_rstd"], 1)
            TT(stat[:, 9:10], stat[:, 8:9], v["gamma"], ALU.mult).then_inc(g["bn_a"], 1)
            dve.wait_ge(g["bn_a"], 1)
            STT(stat[:, 10:11], stat[:, 5:6], stat[:, 9:10], v["beta"], ALU.mult, ALU.add).then_inc(g["bn_b"], 1)
            dve.wait_ge(g["bn_b"], 1)
            flat = wx[:].rearrange("p s b c -> p (s b c)")
            TS(flat, flat, stat[:, 9:10], stat[:, 10:11], ALU.mult, ALU.add).then_inc(g["bn_done"], 1)

            def new_starts(dst, ends, last_sem):
                nc.vector.tensor_copy(dst[:, :, 1:CH], ys[:, L - 1, :, 0:CH - 1])
                nc.vector.tensor_copy(dst[:, :, 0], S[:, 0, 0:B]).then_inc(last_sem, 1)

            dve.wait_ge(g["gram_mm"], 1)
            nc.vector.tensor_reduce(stat[:, 11:12], S[:, 2, 0:P], AX_X, ALU.add, apply_absolute_value=True).then_inc(g["gram_sum"], 1)
            dve.wait_ge(g["gram_sum"], 1)
            TS(stat[:, 14:15], stat[:, 11:12], 1.0 / GRAM_LIMIT, None, ALU.mult).then_inc(g["gram_share"], 1)
            dve.wait_ge(g["ends_mm"], 1)
            new_starts(y0, None, g["y0_done"])
            dve.wait_ge(g["ends_mm"], 2)
            new_starts(y0n, None, g["y0_moved"])
            dve.wait_ge(g["y0_moved"], 1)
            TT(ydiff[:], y0n[:], y0[:], ALU.subtract).then_inc(g["ydiff_a"], 1)
            dve.wait_ge(g["ydiff_a"], 1)
            nc.vector.tensor_reduce(stat[:, 15:16], ydiff[:].rearrange("p b c -> p (b c)"), AX_X, ALU.max,
                                    apply_absolute_value=True).then_inc(g["ydiff_m"], 1)
            dve.wait_ge(g["ydiff_m"], 1)
            STT(stat[:, 12:13], stat[:, 15:16], 1.0 / START_TOL, stat[:, 14:15], ALU.mult, ALU.max).then_inc(g["ydiff_b"], 1)
            dve.wait_ge(g["dmax_t"], 1)
            nc.vector.tensor_reduce(stat[0:1, 13:14], S[0:1, 1, 0:P], AX_X, ALU.max).then_inc(g["flag_a"], 1)
            dve.wait_ge(g["flag_a"], 1)
            TS(flag[0:1, 0:1], stat[0:1, 13:14], 1.0, None, ALU.is_gt)
            nc.vector.tensor_copy(y0[:], y0n[:]).then_inc(g["flag_b"], 1)
            dve.wait_ge(g["flag_b"], 1)
            moved = dve.value_load(flag[0:1, 0:1])
            with dve.If(moved):
                with dve.Fori(0, ALL_PASSES) as i:
                    dve.wait_ge(g["xends_mm"], i + 1)
                    new_starts(y0, None, g["xy0_done"])
            TT(res[:].rearrange("p b (c s) -> p b c s", s=L), ys[:].rearrange("p s b c -> p b c s"),
               x3[:].rearrange("p b (c s) -> p b c s", s=L), ALU.add).then_inc(g["res_done"], 1)


_PLAIN = ["x"] + CONSTS + WEIGHTS + ["vectors"]


def kernel(**inputs):
    import numpy as np
    import concourse.bacc as bacc
    from concourse.bass_utils import run_bass_kernel_spmd

    f = np.float32
    g = {k: np.asarray(x) for k, x in inputs.items()}

    def both(m):
        o = np.zeros((2 * m.shape[0], 2 * m.shape[1]), m.dtype)
        o[:m.shape[0], :m.shape[1]] = m
        o[m.shape[0]:, m.shape[1]:] = m
        return o

    def twice(x):
        return np.concatenate([x, x])

    pp = np.arange(P)
    arr = {"ident": np.eye(P, dtype=f)}
    arr["mean_c"] = both(np.full((C, C), 1.0 / C, f))
    arr["mean_all"] = (pp[:, None] % C == pp[None] % C).astype(f) / f(B * N)
    arr["shift_half"] = (pp[:, None] + C == pp[None]).astype(f)
    arr["den_select"] = (pp[:, None] == pp[None] // HP * HP + HD).astype(f)
    q, k = (pp % (H1 * TQ)) % TQ, np.arange(GK)
    ok = (k[None] >= q[:, None]) & (k[None] - q[:, None] < W)
    arr["window_mask"] = np.tile(np.where(ok, 0.0, -1e30).astype(f), (1, 8))
    col = np.arange(BQ)
    q = col // (H1 * TQ) * TQ + col % TQ
    ok = (pp[:, None] // 2 >= q[None]) & (pp[:, None] // 2 - q[None] < W)
    arr["block_mask"] = np.tile(np.where(ok, 1e30, 0.0).astype(f), (1, BPS))
    row = np.arange(PARTS * 2 * UPG)
    unit, half = row % (2 * UPG) // 2, row % 2
    arr["unit_select"] = ((unit[:, None, None] == np.arange(UPG)[None, :, None])
                          & (half[:, None, None] == (pp % 2)[None, None])).astype(f)
    arr["block_ones"] = (pp[:, None] % 2 == pp[None] // C).astype(f)
    arr["part_scale"] = np.stack([-(pp >= 32).astype(f), -(pp >= 64).astype(f)], 1)

    arr["x"] = np.ascontiguousarray(g["x"].reshape(B, C, N))
    wqkv = g["L0_conv_qkv_w"]
    arr["wq"], arr["wk"], arr["wv"] = (both(wqkv[i * C:(i + 1) * C].T) for i in range(3))
    wp = np.zeros((P, C), f)
    for h in range(H0):
        wp[h * HP:h * HP + HD] = g["L0_conv_proj_w"].T[h * HD:(h + 1) * HD]
    arr["wproj"] = wp
    w1 = np.zeros((P, 2, P), f)
    for half in range(2):
        w1[half * C:(half + 1) * C, half] = g["L0_conv_fc1_w"].T
    arr["wfc1"] = w1
    arr["wfc2"] = np.ascontiguousarray(g["L0_conv_fc2_w"].T)

    def padded(m):
        return np.concatenate([m, np.zeros_like(m)])
    for n, w in (("w1q", "L1_attn_Wq"), ("w1k", "L1_attn_Wk"), ("w1v", "L1_attn_Wv")):
        arr[n] = padded(np.ascontiguousarray(g[w].reshape(H1, C, C).transpose(1, 0, 2)))
    arr["w1u"] = padded(np.ascontiguousarray(g["L1_attn_Wu"].T.reshape(H1, C, C).transpose(1, 0, 2)))
    arr["w_in"] = both(g["L1_ffn_W"].T)
    arr["v_rec"] = both(g["L1_ffn_V"].T)
    vecs = {"ln1_w": "L0_conv_ln1_w", "ln1_b": "L0_conv_ln1_b", "proj_b": "L0_conv_proj_b", "ln2_w": "L0_conv_ln2_w",
            "ln2_b": "L0_conv_ln2_b", "fc2_b": "L0_conv_fc2_b", "attn_b": "L1_attn_bu", "gamma": "L1_ffn_gamma",
            "beta": "L1_ffn_beta"}
    arr["vectors"] = np.stack([g["L0_conv_fc1_b"] if n == "fc1_b" else twice(g[vecs[n]]) for n in VECTORS], 1)

    nc = bacc.Bacc("TRN2", target_bir_lowering=False, num_devices=1)
    arrays, aps = {}, {}
    for n in _PLAIN:
        arrays[n] = np.ascontiguousarray(arr[n])
        aps[n] = nc.dram_tensor(n, arrays[n].shape, mybir.dt.from_np(arrays[n].dtype), kind="ExternalInput").ap()
    out = nc.dram_tensor("result", (B, C, N), F32, kind="ExternalOutput").ap()
    build(nc, aps, out)
    r = run_bass_kernel_spmd(nc, [arrays], core_ids=[0])
    return r.results[0]["result"].reshape(B, C, 32, 32)
```

```python
from contextlib import ExitStack

import concourse.bass as bass
from concourse import mybir

F32 = mybir.dt.float32
BF16 = mybir.dt.bfloat16
I32 = mybir.dt.int32
ALU = mybir.AluOpType
ACT = mybir.ActivationFunctionType
AX_X = mybir.AxisListType.X

P = 128
B, C, N = 4, 64, 1024
HALF = N // 2
H0 = 4
HD = C // H0
HP = P // H0
KT = N // P
PARTS = 3
QTERM = (0, 0, 0, 1, 1, 2)
KTERM = (0, 1, 2, 0, 1, 0)
TERMS = len(QTERM)
KQ = TERMS * HD
QT = KT // 2
ROWS = H0 * QT
PIECES = ROWS * 2
UNITS = KT * 2

H1 = 8
W = 32
TQ = 4
TG = HALF // TQ
NG = P // (H1 * TQ)
GU = TG // NG
GK = W + TQ
BLOCKS = HALF // W
BK = 2 * W
BQ = H1 * W
PAD = W - 1
XW = HALF + W
STAGES = 8
TOKS = 4
BPS = BLOCKS // STAGES
UPS = GU // STAGES
GSEL = 2
UPG = GU // GSEL

L = 16
CH = HALF // L
COLS = B * CH
WARM = 12
ALL_PASSES = 2 * CH
START_TOL = 2.0 ** -22
GRAM_LIMIT = 4.0

CONSTS = ["ident", "mean_c", "mean_all", "shift_half", "den_select", "window_mask", "block_mask",
          "unit_select", "block_ones", "part_scale"]
WEIGHTS = ["wq", "wk", "wv", "wproj", "wfc1", "wfc2", "w1q", "w1k", "w1v", "w1u", "w_in", "v_rec"]
VECTORS = ["ln1_w", "ln1_b", "proj_b", "ln2_w", "ln2_b", "fc1_b", "fc2_b", "attn_b", "gamma", "beta"]


def layernorm_stages(b, which):
    return [(n, b, which) for n in ("ln_mean", "ln_square", "ln_var", "ln_scale")]


def project_stages(b):
    return [*layernorm_stages(b, 1), ("project", b), ("split", b)]


def max_stages(b, half, units):
    pieces = [("max_piece", b, half, i) for i in range(PIECES)]
    per = -(-PIECES // (units - 1))
    out = [pieces[i * per:(i + 1) * per] for i in range(units - 1)]
    return out + [[("max_neg", b, half), ("max_rows", b, half), ("max_parts", b, half)]]


def rest_stages(b):
    out = [("den", b), ("den_exp", b), ("o_norm", b), ("proj", b), *layernorm_stages(b, 2), ("fc1", b), ("fc2", b),
           *layernorm_stages(b, 3), ("keys", b)]
    out.append(("round", b))
    for h in range(H1):
        out.append(("queries", b, h))
        if h:
            out.append(("round_query", b, h - 1))
    out += [("tokens", b, 0), ("round_query", b, H1 - 1)] + [("tokens", b, r) for r in range(1, TOKS)]
    out += [("windows", b, r) for r in range(STAGES)]
    out += [("win_max", b), ("win_rows", b), ("win_parts", b), ("blk_scores", b, 0), ("blk_mask", b, 0)]
    for r in range(STAGES):
        if r + 1 < STAGES:
            out.append(("blk_scores", b, r + 1))
        out.append(("blk_den", b, r))
        if r + 1 < STAGES:
            out.append(("blk_mask", b, r + 1))
        out.append(("blk_out", b, r))
    out += [("unify", b, h) for h in range(0, H1, 2)]
    return out + [*layernorm_stages(b, 4), ("wx", b)]


def attend_stages(b):
    out = []
    for half in range(2):
        if half == 0:
            ahead = max_stages(b, 1, KT)
        else:
            ahead = max_stages(b + 1, 0, KT) if b + 1 < B else [[] for _ in range(KT)]
        for j in range(KT):
            u = half * KT + j
            pieces = ahead[j]
            k = len(pieces) // 2
            out += [("scores", b, u, 0), *pieces[:k], ("scores", b, u, 1), *pieces[k:]]
            if u:
                out.append(("values", b, u - 1))
    return out + [("values", b, UNITS - 1)]


ROOM = {"ln_mean": 3.0, "ln_square": 2.0, "ln_var": 3.0, "ln_scale": 2.0, "den": 3.0, "den_exp": 2.0, "o_norm": 3.0,
        "proj": 2.0, "fc1": 3.0, "fc2": 3.0, "keys": 3.0, "round": 0.0, "round_query": 0.0, "queries": 1.0, "tokens": 1.0, "windows": 1.0,
        "win_max": 4.0, "win_rows": 3.0, "win_parts": 3.0, "blk_scores": 1.0, "blk_mask": 0.5, "blk_den": 1.0, "blk_out": 0.5,
        "unify": 0.25, "wx": 1.0}


def order_of_stages():
    out = [*project_stages(0), *(x for unit in max_stages(0, 0, 2) for x in unit)]
    for b in range(B):
        main = attend_stages(b)
        first = project_stages(b + 1) if b + 1 < B else []
        other = rest_stages(b - 1) if b else []
        start = 3 * len(first)
        room = [ROOM.get(name, 1.0) for name, *_ in other]
        done = 0
        for i, x in enumerate(main):
            out.append(x)
            if i % 3 == 2 and i < start:
                out.append(first[i // 3])
            share = sum(room) * max(0, i + 1 - start) / (len(main) - start)
            while done < len(other) and sum(room[:done + 1]) <= share + 1e-6:
                out.append(other[done])
                done += 1
        out += other[done:]
    return out + rest_stages(B - 1)


def build(nc, a, out):
    with ExitStack() as ctx:
        def sb(name, shape, dt=F32):
            return ctx.enter_context(nc.sbuf_tensor(name, shape, dt))

        def sem(name):
            return ctx.enter_context(nc.semaphore(name))

        shape_of = {n: list(a[n].shape) for n in CONSTS + WEIGHTS}
        early = {"w1q", "w1k", "w1v", "w1u", "unit_select"}
        t = {n: sb("s_" + n, shape_of[n]) for n in CONSTS + WEIGHTS if n not in early}
        vec = sb("vec", [P, len(VECTORS)])
        v = {n: vec[:, i:i + 1] for i, n in enumerate(VECTORS)}
        eps = sb("eps", [P, 1])
        unit_sel = sb("unit_sel", [PARTS * 2 * UPG, UPG, P], BF16)
        abd = sb("abd", [P, H1, P])
        gbd = sb("gbd", [P, H1, P])

        X = sb("X", [P, B, HALF])
        ln_d = sb("ln_d", [P, HALF])
        ln_q = sb("ln_q", [P, HALF])
        ln_l = sb("ln_l", [P, HALF])
        ln_r = sb("ln_r", [P, HALF])
        ln_y = sb("ln_y", [P, HALF])
        x_ln = sb("x_ln", [P, HALF])
        qk_part = sb("qk_part", [P, PARTS, 2, HALF], BF16)
        qk_rest = sb("qk_rest", [P, 2, HALF])
        QX = [sb(f"QX{i}", [KQ + PARTS, 2, H0, HALF], BF16) for i in range(2)]
        KX = [sb(f"KX{i}", [KQ + PARTS, 2, H0, HALF], BF16) for i in range(2)]
        VT = [sb(f"VT{i}", [P, KT, H0, HP]) for i in range(2)]
        part_max = sb("part_max", [P, ROWS, 2])
        neg_max = sb("neg_max", [P, PARTS, ROWS])
        mx_hi = sb("mx_hi", [PARTS * ROWS, P], BF16)
        mx_rest = sb("mx_rest", [PARTS * ROWS, P])
        mx_mid = sb("mx_mid", [PARTS * ROWS, P], BF16)
        mx_part = sb("mx_part", [PARTS * ROWS, P], BF16)
        rlog = sb("rlog", [P, 2, HALF])
        probs = sb("probs", [P, 2, H0, HALF])
        o_sb = sb("o_sb", [P, 2, HALF])
        rden = sb("rden", [P, 2, HALF])
        o_norm = sb("o_norm", [P, 2, HALF])
        x1 = sb("x1", [P, HALF])
        hid = o_norm
        x2 = sb("x2", [P, HALF])

        xh = sb("xh", [P, HALF])
        xbd = sb("xbd", [P, XW, 2])
        xbd16 = sb("xbd16", [P, 2, XW], BF16)
        z = sb("z", [P, TG, H1, TQ])
        zs = sb("zs", [P, GU * 2 * GK + TG * H1 * TQ // 2])
        z16 = zs[:, 0:TG * H1 * TQ // 2].bitcast(BF16).rearrange("p (t h q) -> p t h q", h=H1, q=TQ)
        s_win = zs[:, TG * H1 * TQ // 2:].rearrange("p (s k) -> p s k", k=GK)
        y1 = zs[:, 0:H1 * TG * TQ].rearrange("p (h t q) -> p h t q", h=H1, q=TQ)
        x_tok = sb("x_tok", [P, BLOCKS, P])
        neg_m1 = sb("neg_m1", [P, GSEL, PARTS, 2 * UPG])
        m1_hi = sb("m1_hi", [PARTS * 2 * UPG, GSEL, P], BF16)
        m1_rest = sb("m1_rest", [PARTS * 2 * UPG, GSEL, P])
        m1_mid = sb("m1_mid", [PARTS * 2 * UPG, GSEL, P], BF16)
        m1_part = sb("m1_part", [PARTS * 2 * UPG, GSEL, P], BF16)
        p1 = sb("p1", [P, 2, BPS * BQ])
        x3 = sb("x3", [P, B, HALF])
        y1_flat = zs[:, 0:H1 * TG * TQ]
        for i, n in enumerate(("w1q", "w1k", "w1v", "w1u")):
            t[n] = y1_flat[:, i * H1 * C:(i + 1) * H1 * C].rearrange("p (h m) -> p h m", h=H1)
        t["unit_select"] = x_tok[0:PARTS * 2 * UPG, 0:UPG, :]

        wx = sb("wx", [P, L, B, CH])
        ys = probs[:, 0, :, :].rearrange("p a n -> p (a n)").rearrange("p (s b c) -> p s b c", s=L, b=B)
        y0 = sb("y0", [P, B, CH])
        y0n = sb("y0n", [P, B, CH])
        ydiff = sb("ydiff", [P, B, CH])
        stat = sb("stat", [P, 16])
        flag = sb("flag", [1, 2], I32)
        res = probs[:, 1, :, :]

        S = ctx.enter_context(nc.psum_tensor("S", [P, 2, 512], F32))
        O = ctx.enter_context(nc.psum_tensor("O", [P, 512], F32))
        R = ctx.enter_context(nc.psum_tensor("R", [P, 3, 512], F32))
        M = ctx.enter_context(nc.psum_tensor("M", [P, 2, 512], F32))

        scratch = nc.dram_tensor("qk_scratch", [B, PARTS, 2, H0, HD, N], BF16, kind="Internal").ap()

        names = """consts_in x_in weights_in fills pool_fills ones_rows unit_sel_done abd_mm gbd_mm abd_done
            ln_mean ln_ctr ln_sq ln_var ln_log ln_rstd ln_norm ln_out
            qk_mm v_mm qk_hi qk_rst qk_mid qk_lo qk_dram qk_in v_copied
            max_mm max_red negmax negmax_t mx_h mx_r mx_m mx_done shift_in
            st_mm exp_done pv_mm o_copied den_mm den_log rden_done o_normed proj_mm x1_done
            fc1_mm gelu_done fc2_mm x2_done
            shift_mm xbd_a xbd_pad xbd_cast z_mm z_copied z_cast tok_mm tok_copied
            sw_mm sw_masked sw_max m1_rep m1_t m1_h m1_r m1_m m1_done
            s1_mm p1_exp p1_masked den1_mm den1_log rden1_done pv1_mm y1_done fin_mm x3_done
            wx_mm wx_copied wsum mean_mm mean_done sqs var_mm bn_log bn_rstd bn_a bn_b bn_done
            gram_mm gram_sum gram_share ydiff_m pre_mm y_done ends_mm y0_moved y0_done ydiff_a ydiff_b
            dmax_t flag_a flag_b xpre_mm xy_done xends_mm xy0_done res_done out_done""".split()
        g = {n: sem(n) for n in names}

        def half_rows(h):
            return slice(h * C, (h + 1) * C)

        timeline = order_of_stages()
        lns = [a for name, *a in timeline if name == "ln_mean"]
        affine = [a for a in lns if a[1] in (1, 2)]

        def ln_no(b, which):
            return lns.index([b, which])

        def ln_in(b, which):
            return {1: X[:, b, :], 2: x1[:, :], 3: x2[:, :], 4: x3[:, b, :]}[which]

        def ln_banks(which):
            return (1, 2) if which == 4 else (0, 1)

        def run(stages):
            for name, *args in timeline:
                if name in stages:
                    stages[name](*args)

        block = ctx.enter_context(nc.Block())

        @block.sync
        def _(sp):
            for half in range(2):
                sp.dma_start(X[half_rows(half), :, :],
                             a["x"][:, :, half * HALF:(half + 1) * HALF].rearrange("b c n -> c b n")).then_inc(g["x_in"], 16)
            for n in CONSTS:
                src = a[n]
                sp.dma_start(t[n][:] if n not in early else t[n], src).then_inc(g["consts_in"], 16)
            for n in WEIGHTS:
                sp.dma_start(t[n][:] if n not in early else t[n], a[n]).then_inc(g["weights_in"], 16)
            sp.dma_start(vec[:, :], a["vectors"]).then_inc(g["weights_in"], 16)

            def relayout(b):
                sp.wait_ge(g["qk_lo"], b + 1)
                for half in range(2):
                    sp.dma_start(scratch[b].rearrange("p q h d n -> (h d) p q n")[:, :, :, half * HALF:(half + 1) * HALF],
                                 qk_part[half_rows(half), :, :, :]).then_inc(g["qk_dram"], 16)
                sp.wait_ge(g["qk_dram"], 32 * (b + 1))
                if b >= 2:
                    sp.wait_ge(g["st_mm"], 2 * UNITS * (b - 1))
                for r in range(TERMS):
                    for q, (dst, part) in enumerate(((QX[b % 2], QTERM[r]), (KX[b % 2], KTERM[r]))):
                        for half in range(2):
                            sp.dma_start(dst[r * HD:(r + 1) * HD, half, :, :],
                                         scratch[b, part, q].rearrange("h d n -> d h n")[:, :, half * HALF:(half + 1) * HALF]
                                         ).then_inc(g["qk_in"], 16)

            def shift_rows(b, half):
                sp.wait_ge(g["mx_done"], 2 * b + half + 1)
                for p in range(PARTS):
                    sp.dma_start(QX[b % 2][KQ + p:KQ + p + 1, half, :, :].rearrange("o h (t n) -> o (h t) n", n=P),
                                 mx_part[p * ROWS:(p + 1) * ROWS, :]).then_inc(g["shift_in"], 16)

            run({"split": relayout, "max_parts": shift_rows})
            sp.wait_ge(g["res_done"], 1)
            for half in range(2):
                sp.dma_start(out[:, :, half * HALF:(half + 1) * HALF].rearrange("b c n -> c b n"),
                             res[half_rows(half), :, :]).then_inc(g["out_done"], 16)
            sp.wait_ge(g["out_done"], 32)

        @block.gpsimd
        def _(pool):
            def copy(dst, src):
                return nc.gpsimd.tensor_scalar(dst, src, 1.0, None, ALU.mult)

            nc.gpsimd.memset(eps[:], 1e-5)
            nc.gpsimd.memset(xbd[:], 0.0)
            for i in range(2):
                nc.gpsimd.memset(VT[i][:], 0.0).then_inc(g["pool_fills"], 1)
            pool.wait_ge(g["pool_fills"], 2)
            for i in range(2):
                nc.gpsimd.memset(VT[i][:, :, :, HD:HD + 1], 1.0).then_inc(g["pool_fills"], 1)
            nc.gpsimd.memset(y0[:], 0.0).then_inc(g["pool_fills"], 1)
            pool.wait_ge(g["consts_in"], 16 * len(CONSTS))
            pool.wait_ge(g["pool_fills"], 5)
            copy(unit_sel[:], t["unit_select"]).then_inc(g["unit_sel_done"], 1)

            def split(b):
                pool.wait_ge(g["qk_rst"], b + 1)
                if b:
                    pool.wait_ge(g["qk_dram"], 32 * b)
                copy(qk_part[:, 1], qk_rest[:, :, :]).then_inc(g["qk_mid"], 1)
                pool.wait_ge(g["qk_mid"], b + 1)
                nc.gpsimd.tensor_tensor(qk_part[:, 2], qk_rest[:, :, :], qk_part[:, 1], ALU.subtract).then_inc(g["qk_lo"], 1)

            def o_norm_(b):
                pool.wait_ge(g["rden_done"], b + 1)
                pool.wait_ge(g["o_copied"], 2 * (b + 1))
                nc.gpsimd.tensor_tensor(o_norm[:], o_sb[:], rden[:], ALU.mult).then_inc(g["o_normed"], 1)

            def keys(b):
                pool.wait_ge(g["ln_norm"], ln_no(b, 3) + 1)
                if b:
                    pool.wait_ge(g["s1_mm"], STAGES * b)
                copy(xbd[0:C, PAD:PAD + HALF, 0], xh[0:C, :])
                copy(xbd[C:P, PAD:PAD + HALF, 1], xh[C:P, :]).then_inc(g["xbd_a"], 1)

            def round_(b):
                pool.wait_ge(g["xbd_a"], b + 1)
                pool.wait_ge(g["xbd_pad"], b + 1)
                if b:
                    pool.wait_ge(g["sw_mm"], STAGES * b)
                copy(xbd16[:], xbd[:].rearrange("p k a -> p a k")).then_inc(g["xbd_cast"], 1)

            run({"split": split, "o_norm": o_norm_, "keys": keys, "round": round_})

        @block.tensor
        def _(pe):
            mm = nc.tensor.matmul

            def ln_mean(b, which):
                if which == 1 and b >= 3:
                    pe.wait_ge(g["wx_copied"], b - 2)
                elif which == 1 and b:
                    pe.wait_ge(g["qk_rst"], b)
                elif which == 2:
                    pe.wait_ge(g["x1_done"], b + 1)
                elif which == 3:
                    pe.wait_ge(g["x2_done"], b + 1)
                elif which == 4:
                    pe.wait_ge(g["x3_done"], b + 1)
                mm(R[:, ln_banks(which)[0], :], t["mean_c"][:], ln_in(b, which), start=True, stop=True).then_inc(g["ln_mean"], 1)

            def ln_var(b, which):
                pe.wait_ge(g["ln_sq"], ln_no(b, which) + 1)
                mm(R[:, ln_banks(which)[1], :], t["mean_c"][:], ln_q[:], start=True, stop=True).then_inc(g["ln_var"], 1)

            def project(b):
                pe.wait_ge(g["ln_out"], affine.index([b, 1]) + 1)
                mm(R[:, 0, :], t["wq"][:], x_ln[:], start=True, stop=True)
                mm(R[:, 1, :], t["wk"][:], x_ln[:], start=True, stop=True).then_inc(g["qk_mm"], 1)
                if b == 1:
                    pe.wait_ge(g["v_copied"], 1)
                for j in range(QT):
                    last = mm(R[:, 2, j * P:(j + 1) * P], x_ln[:, j * P:(j + 1) * P], t["wv"][:], start=True, stop=True)
                last.then_inc(g["v_mm"], 1)

            def max_piece(b, half, i):
                h, rest = divmod(i, QT * 2)
                nt, kh = divmod(rest, 2)
                hn = 2 * b + half
                n = hn * PIECES + i
                if i == 0:
                    pe.wait_ge(g["qk_in"], 16 * 4 * TERMS * (b + 1))
                    if hn:
                        pe.wait_ge(g["mx_r"], hn)
                if n >= 2:
                    pe.wait_ge(g["max_red"], n - 1)
                mm(M[:, n % 2, :], QX[b % 2][0:KQ, half, h, nt * P:(nt + 1) * P], KX[b % 2][0:KQ, kh, h, :],
                   start=True, stop=True).then_inc(g["max_mm"], 1)

            def max_rows(b, half):
                pe.wait_ge(g["negmax"], 2 * b + half + 1)
                mm(M[0:PARTS * ROWS, 0, 0:P], neg_max[:], t["ident"][:], start=True, stop=True).then_inc(g["negmax_t"], 1)

            def scores(b, u, pair):
                half, j = divmod(u, KT)
                n = (b * UNITS + u) * 2 + pair
                if j == 0 and pair == 0:
                    pe.wait_ge(g["shift_in"], 16 * PARTS * (2 * b + half + 1))
                if n:
                    pe.wait_ge(g["exp_done"], n)
                for k in range(2):
                    h = pair * 2 + k
                    last = mm(S[:, k, :], KX[b % 2][:, j // QT, h, j % QT * P:(j % QT + 1) * P], QX[b % 2][:, half, h, :],
                              start=True, stop=True)
                last.then_inc(g["st_mm"], 1)

            def values(b, u):
                half, j = divmod(u, KT)
                n = b * UNITS + u
                if u == 0:
                    pe.wait_ge(g["v_copied"], b + 1)
                if j == 0 and n:
                    pe.wait_ge(g["o_copied"], 2 * b + half)
                pe.wait_ge(g["exp_done"], 2 * (n + 1))
                for h in range(H0):
                    last = mm(O[h * HP:(h + 1) * HP, :], VT[b % 2][:, j, h, :], probs[:, u % 2, h, :],
                              start=(j == 0), stop=(j == KT - 1))
                last.then_inc(g["pv_mm"], 1)

            def den(b):
                pe.wait_ge(g["o_copied"], 2 * (b + 1))
                if b + 2 < B:
                    pe.wait_ge(g["qk_rst"], b + 3)
                elif b:
                    pe.wait_ge(g["wx_copied"], b)
                for half in range(2):
                    last = mm(R[:, half, :], t["den_select"][:], o_sb[:, half, :], start=True, stop=True)
                last.then_inc(g["den_mm"], 1)

            def proj(b):
                pe.wait_ge(g["o_normed"], b + 1)
                if b + 2 < B:
                    pe.wait_ge(g["v_copied"], b + 3)
                for half in range(2):
                    last = mm(R[half_rows(half), 2, :], t["wproj"][:], o_norm[:, half, :], start=True, stop=True)
                last.then_inc(g["proj_mm"], 1)

            def fc1(b):
                pe.wait_ge(g["ln_out"], affine.index([b, 2]) + 1)
                for half in range(2):
                    last = mm(R[:, half, :], t["wfc1"][:, half, :], x_ln[:], start=True, stop=True)
                last.then_inc(g["fc1_mm"], 1)

            def fc2(b):
                pe.wait_ge(g["gelu_done"], b + 1)
                for half in range(2):
                    last = mm(R[half_rows(half), 2, :], t["wfc2"][:], hid[:, half, :], start=True, stop=True)
                last.then_inc(g["fc2_mm"], 1)

            def keys(b):
                pe.wait_ge(g["ln_norm"], ln_no(b, 3) + 1)
                mm(R[:, 2, 0:PAD], t["shift_half"][:], xh[:, HALF - PAD:HALF], start=True, stop=True).then_inc(g["shift_mm"], 1)

            def queries(b, h):
                if h == 2:
                    pe.wait_ge(g["xbd_pad"], b + 1)
                elif h >= 3:
                    pe.wait_ge(g["z_copied"], b * H1 + h - 2)
                mm(R[:, h % 3, :], abd[:, h, :], xh[:], start=True, stop=True).then_inc(g["z_mm"], 1)

            def tokens(b, r):
                pe.wait_ge(g["z_copied"], b * H1 + min(H1, 6 + r))
                if r == 0:
                    pe.wait_ge(g["xbd_a"], b + 1)
                elif r == 3:
                    pe.wait_ge(g["tok_copied"], b * TOKS + 1)
                for k in range(BLOCKS // TOKS):
                    i = r * (BLOCKS // TOKS) + k
                    last = nc.tensor.transpose(R[:, (2 + r) % 3, k * P:(k + 1) * P],
                                               xbd[:, i * W:i * W + BK, :].rearrange("p k a -> p (k a)"), t["ident"][:])
                last.then_inc(g["tok_mm"], 1)

            def windows(b, r):
                if r == 0:
                    pe.wait_ge(g["xbd_cast"], b + 1)
                    pe.wait_ge(g["z_cast"], H1 * (b + 1))
                if r < 3:
                    pe.wait_ge(g["tok_copied"], b * TOKS + 2 + r)
                else:
                    pe.wait_ge(g["sw_masked"], b * STAGES + r - 2)
                for k in range(UPS):
                    for gi in range(NG):
                        tg = (r * UPS + k) * NG + gi
                        last = mm(R[gi * 32:(gi + 1) * 32, r % 3, k * 2 * GK:(k + 1) * 2 * GK], z16[:, tg, :, :],
                                  xbd16[:, :, tg * TQ:tg * TQ + GK], start=True, stop=True)
                last.then_inc(g["sw_mm"], 1)

            def win_rows(b):
                pe.wait_ge(g["m1_rep"], b + 1)
                for gs in range(GSEL):
                    last = mm(R[0:PARTS * 2 * UPG, 2, gs * P:(gs + 1) * P], neg_m1[:, gs, :, :], t["ident"][:], start=True, stop=True)
                last.then_inc(g["m1_t"], 1)

            def blk_scores(b, r):
                n = b * STAGES + r
                if r == 0:
                    pe.wait_ge(g["m1_done"], b + 1)
                else:
                    pe.wait_ge(g["p1_exp"], n)
                for k in range(BPS):
                    i = r * BPS + k
                    mm(R[:, 0, k * BQ:(k + 1) * BQ], xbd[:, i * W:i * W + BK, :].rearrange("p k a -> p (k a)"),
                       z[:, i * 8:(i + 1) * 8, :, :], start=True, stop=False)
                    for uu in range(2):
                        u = 2 * i + uu
                        last = mm(R[:, 0, k * BQ + uu * P:k * BQ + (uu + 1) * P], unit_sel[:, u % UPG, :], m1_part[:, u // UPG, :],
                                  start=False, stop=(uu == 1))
                last.then_inc(g["s1_mm"], 1)

            def blk_den(b, r):
                n = b * STAGES + r
                pe.wait_ge(g["p1_masked"], n + 1)
                if n:
                    pe.wait_ge(g["den1_log"], n)
                mm(R[:, 1, :], t["block_ones"][:], p1[:, r % 2, :], start=True, stop=True).then_inc(g["den1_mm"], 1)
                if n:
                    pe.wait_ge(g["y1_done"], n)
                for k in range(BPS):
                    last = mm(R[:, 2, k * BQ:(k + 1) * BQ], x_tok[:, r * BPS + k, :], p1[:, r % 2, k * BQ:(k + 1) * BQ],
                              start=True, stop=True)
                last.then_inc(g["pv1_mm"], 1)

            def unify(b, h0):
                if h0 == 0:
                    pe.wait_ge(g["y1_done"], (b + 1) * STAGES)
                for h in range(h0, h0 + 2):
                    last = mm(R[:, 0, :], gbd[:, h, :], y1[:, h, :, :], start=(h == 0), stop=(h == H1 - 1))
                if h0 + 2 == H1:
                    last.then_inc(g["fin_mm"], 1)

            def wx_(b):
                pe.wait_ge(g["ln_norm"], ln_no(b, 4) + 1)
                mm(R[:, 0, :], t["w_in"][:], xh[:], start=True, stop=True).then_inc(g["wx_mm"], 1)

            pe.wait_ge(g["x_in"], 32)
            pe.wait_ge(g["consts_in"], 16 * len(CONSTS))
            pe.wait_ge(g["weights_in"], 16 * (len(WEIGHTS) + 1))
            for h in range(H1):
                for half in range(2):
                    last = mm(S[half_rows(half), h // 4, (h % 4) * P + half * C:(h % 4) * P + (half + 1) * C],
                              t["w1q"][:, h, :], t["w1k"][:, h, :], start=True, stop=True)
            last.then_inc(g["abd_mm"], 1)
            for h in range(H1):
                for half in range(2):
                    last = mm(M[half_rows(half), h // 4, (h % 4) * P + half * C:(h % 4) * P + (half + 1) * C],
                              t["w1v"][:, h, :], t["w1u"][:, h, :], start=True, stop=True)
            last.then_inc(g["gbd_mm"], 1)
            pe.wait_ge(g["unit_sel_done"], 1)
            pe.wait_ge(g["ones_rows"], 2)
            pe.wait_ge(g["abd_done"], 4)
            run({"ln_mean": ln_mean, "ln_var": ln_var, "project": project, "max_piece": max_piece, "max_rows": max_rows,
                 "scores": scores, "values": values, "den": den, "proj": proj, "fc1": fc1, "fc2": fc2, "keys": keys,
                 "queries": queries, "tokens": tokens, "windows": windows, "win_rows": win_rows, "blk_scores": blk_scores,
                 "blk_den": blk_den, "unify": unify, "wx": wx_})
            pe.wait_ge(g["wx_copied"], B)

            pe.wait_ge(g["wsum"], 1)
            mm(R[:, 0, 0:1], t["mean_all"][:], stat[:, 4:5], start=True, stop=True).then_inc(g["mean_mm"], 1)
            pe.wait_ge(g["sqs"], 1)
            mm(R[:, 1, 0:1], t["mean_all"][:], stat[:, 6:7], start=True, stop=True).then_inc(g["var_mm"], 1)
            pe.wait_ge(g["bn_done"], 1)

            def rnn_step(step, prev, wait_prev, signal):
                bank = M[:, step % 2, 0:COLS]
                mm(bank, t["ident"][:], wx[:, step].rearrange("p b c -> p (b c)"), start=True, stop=False)
                wait_prev()
                mm(bank, t["v_rec"][:], prev.rearrange("p b c -> p (b c)"), start=False, stop=True).then_inc(signal, 1)

            mm(R[:, 2, 0:P], t["v_rec"][:], t["v_rec"][:], start=True, stop=True).then_inc(g["gram_mm"], 1)
            for ps, first in enumerate((L - WARM, 0)):
                for step in range(first, L):
                    n = ps * WARM + step - first

                    def wait_prev(step=step, n=n, first=first, ps=ps):
                        if step > first:
                            pe.wait_ge(g["y_done"], n)
                        elif ps:
                            pe.wait_ge(g["y0_done"], 1)
                    if n >= 2:
                        pe.wait_ge(g["y_done"], n - 1)
                    rnn_step(step, ys[:, step - 1] if step > first else y0[:], wait_prev, g["pre_mm"])
                pe.wait_ge(g["y_done"], n + 1)
                mm(R[:, 0, 0:B], t["shift_half"][:], ys[:, L - 1, :, CH - 1], start=True, stop=True).then_inc(g["ends_mm"], 1)
            pe.wait_ge(g["ydiff_b"], 1)
            mm(R[0:1, 1, 0:P], stat[:, 12:13], t["ident"][:], start=True, stop=True).then_inc(g["dmax_t"], 1)
            pe.wait_ge(g["flag_b"], 1)
            moved = pe.value_load(flag[0:1, 0:1])
            with pe.If(moved):
                with pe.Fori(0, ALL_PASSES) as i:
                    for step in range(L):
                        if step >= 2:
                            pe.wait_ge(g["xy_done"], i * L + step - 1)

                        def wait_prev(step=step):
                            if step:
                                pe.wait_ge(g["xy_done"], i * L + step)
                        rnn_step(step, ys[:, step - 1] if step else y0[:], wait_prev, g["xpre_mm"])
                    pe.wait_ge(g["xy_done"], i * L + L)
                    mm(R[:, 0, 0:B], t["shift_half"][:], ys[:, L - 1, :, CH - 1], start=True, stop=True).then_inc(g["xends_mm"], 1)
                    pe.wait_ge(g["xy0_done"], i + 1)

        @block.scalar
        def _(act):
            A = nc.scalar.activation

            def ln_square(b, which):
                act.wait_ge(g["ln_ctr"], ln_no(b, which) + 1)
                A(ln_q[:], ln_d[:], ACT.Square).then_inc(g["ln_sq"], 1)

            def ln_var(b, which):
                i = ln_no(b, which)
                act.wait_ge(g["ln_var"], i + 1)
                A(ln_l[:], R[:, ln_banks(which)[1], :], ACT.Ln, bias=eps[:, 0:1]).then_inc(g["ln_log"], 1)
                act.wait_ge(g["ln_log"], i + 1)
                A(ln_r[:], ln_l[:], ACT.Exp, scale=-0.5).then_inc(g["ln_rstd"], 1)

            def project(b):
                act.wait_ge(g["qk_mm"], b + 1)
                if b:
                    act.wait_ge(g["qk_dram"], 32 * b)
                A(qk_part[:, 0], R[:, 0:2, :], ACT.Copy).then_inc(g["qk_hi"], 1)
                act.wait_ge(g["v_mm"], b + 1)
                if b >= 2:
                    act.wait_ge(g["pv_mm"], UNITS * (b - 1))
                for half in range(2):
                    last = A(VT[b % 2][:, half * QT:(half + 1) * QT, :, 0:HD],
                             R[:, 2, :].rearrange("p (j a h d) -> p a j h d", j=QT, a=2, h=H0)[:, half], ACT.Copy)
                last.then_inc(g["v_copied"], 1)

            def scores(b, u, pair):
                n = b * UNITS + u
                if n >= 2 and pair == 0:
                    act.wait_ge(g["pv_mm"], n - 1)
                act.wait_ge(g["st_mm"], 2 * n + pair + 1)
                A(probs[:, u % 2, 2 * pair:2 * pair + 2, :], S[:, :, :], ACT.Exp, scale=HD ** -0.5).then_inc(g["exp_done"], 1)

            def den(b):
                act.wait_ge(g["den_mm"], b + 1)
                A(rlog[:], R[:, 0:2, :], ACT.Ln).then_inc(g["den_log"], 1)

            def den_exp(b):
                act.wait_ge(g["den_log"], b + 1)
                A(rden[:], rlog[:], ACT.Exp, scale=-1.0).then_inc(g["rden_done"], 1)

            def fc1(b):
                act.wait_ge(g["fc1_mm"], b + 1)
                A(hid[:, :, :], R[:, 0:2, :], ACT.Gelu, bias=v["fc1_b"]).then_inc(g["gelu_done"], 1)
                nc.scalar.preload_act_table_set("natural_log_exp_and_others")

            def queries(b, h):
                act.wait_ge(g["z_mm"], b * H1 + h + 1)
                A(z[:, :, h, :], R[:, h % 3, :].rearrange("p (t q) -> p t q", q=TQ), ACT.Copy).then_inc(g["z_copied"], 1)

            def blk_scores(b, r):
                n = b * STAGES + r
                act.wait_ge(g["s1_mm"], n + 1)
                if n >= 2:
                    act.wait_ge(g["pv1_mm"], n - 1)
                A(p1[:, r % 2, :], R[:, 0, :], ACT.Exp).then_inc(g["p1_exp"], 1)

            def blk_den(b, r):
                n = b * STAGES + r
                act.wait_ge(g["den1_mm"], n + 1)
                if n >= 2:
                    act.wait_ge(g["y1_done"], n - 1)
                A(rlog[:, r % 2, :], R[:, 1, :], ACT.Ln).then_inc(g["den1_log"], 1)
                act.wait_ge(g["den1_log"], n + 1)
                A(rden[:, r % 2, :], rlog[:, r % 2, :], ACT.Exp, scale=-1.0).then_inc(g["rden1_done"], 1)

            def wx_(b):
                act.wait_ge(g["wx_mm"], b + 1)
                A(wx[:, :, b, :], R[:, 0, :].rearrange("p (c s) -> p s c", s=L), ACT.Copy,
                  accum_out=stat[:, b:b + 1]).then_inc(g["wx_copied"], 1)

            act.wait_ge(g["pool_fills"], 5)
            nc.scalar.preload_act_table_set("natural_log_exp_and_others")
            act.wait_ge(g["abd_mm"], 1)
            act.wait_ge(g["fills"], 2)
            for half in range(2):
                A(abd[half_rows(half), :, half_rows(half)],
                  S[half_rows(half), :, :].rearrange("p k (h m) -> p (k h) m", h=4)[:, :, half_rows(half)],
                  ACT.Copy, scale=0.125).then_inc(g["abd_done"], 1)
            act.wait_ge(g["gbd_mm"], 1)
            for half in range(2):
                A(gbd[half_rows(half), :, half_rows(half)],
                  M[half_rows(half), :, :].rearrange("p k (h m) -> p (k h) m", h=4)[:, :, half_rows(half)],
                  ACT.Copy).then_inc(g["abd_done"], 1)
            run({"ln_square": ln_square, "ln_var": ln_var, "project": project, "scores": scores, "den": den,
                 "den_exp": den_exp, "fc1": fc1, "queries": queries, "blk_scores": blk_scores, "blk_den": blk_den, "wx": wx_})
            act.wait_ge(g["mean_done"], 1)
            A(res[:].rearrange("p b n -> p (b n)"), wx[:].rearrange("p s b c -> p (s b c)"), ACT.Square,
              bias=stat[:, 5:6], accum_out=stat[:, 6:7]).then_inc(g["sqs"], 1)
            act.wait_ge(g["var_mm"], 1)
            A(stat[:, 7:8], R[:, 1, 0:1], ACT.Ln, bias=eps[:, 0:1]).then_inc(g["bn_log"], 1)
            act.wait_ge(g["bn_log"], 1)
            A(stat[:, 8:9], stat[:, 7:8], ACT.Exp, scale=-0.5).then_inc(g["bn_rstd"], 1)
            nc.scalar.preload_act_table(ACT.Sigmoid)
            for n, step in enumerate([*range(L - WARM, L), *range(L)]):
                act.wait_ge(g["pre_mm"], n + 1)
                A(ys[:, step].rearrange("p b c -> p (b c)"), M[:, step % 2, 0:COLS], ACT.Sigmoid).then_inc(g["y_done"], 1)
            act.wait_ge(g["flag_b"], 1)
            moved = act.value_load(flag[0:1, 0:1])
            with act.If(moved):
                with act.Fori(0, ALL_PASSES) as i:
                    for step in range(L):
                        act.wait_ge(g["xpre_mm"], i * L + step + 1)
                        A(ys[:, step].rearrange("p b c -> p (b c)"), M[:, step % 2, 0:COLS], ACT.Sigmoid).then_inc(g["xy_done"], 1)

        @block.vector
        def _(dve):
            TT, TS, STT = nc.vector.tensor_tensor, nc.vector.tensor_scalar, nc.vector.scalar_tensor_tensor

            def ln_mean(b, which):
                dve.wait_ge(g["ln_mean"], ln_no(b, which) + 1)
                TT(ln_d[:], ln_in(b, which), R[:, ln_banks(which)[0], :], ALU.subtract).then_inc(g["ln_ctr"], 1)

            def ln_scale(b, which):
                i = ln_no(b, which)
                dve.wait_ge(g["ln_rstd"], i + 1)
                TT(ln_y[:] if which < 3 else xh[:], ln_d[:], ln_r[:], ALU.mult).then_inc(g["ln_norm"], 1)
                if which < 3:
                    dve.wait_ge(g["ln_norm"], i + 1)
                    TS(x_ln[:], ln_y[:], v[f"ln{which}_w"], v[f"ln{which}_b"], ALU.mult, ALU.add).then_inc(g["ln_out"], 1)

            def project(b):
                dve.wait_ge(g["qk_hi"], b + 1)
                if b:
                    dve.wait_ge(g["qk_lo"], b)
                TT(qk_rest[:, :, :], R[:, 0:2, :], qk_part[:, 0], ALU.subtract).then_inc(g["qk_rst"], 1)

            def max_piece(b, half, i):
                row, kh = divmod(i, 2)
                n = (2 * b + half) * PIECES + i
                dve.wait_ge(g["max_mm"], n + 1)
                nc.vector.tensor_reduce(part_max[:, row, kh:kh + 1], M[:, n % 2, :], AX_X, ALU.max).then_inc(g["max_red"], 1)

            def max_neg(b, half):
                dve.wait_ge(g["max_red"], (2 * b + half + 1) * PIECES)
                for p in range(PARTS):
                    last = nc.vector.tensor_reduce(neg_max[:, p, :], part_max[:, :, :], AX_X, ALU.max, negate=True)
                last.then_inc(g["negmax"], 1)

            def max_rows(b, half):
                hn = 2 * b + half
                dve.wait_ge(g["negmax_t"], hn + 1)
                nc.vector.tensor_copy(mx_hi[:], M[0:PARTS * ROWS, 0, 0:P]).then_inc(g["mx_h"], 1)
                dve.wait_ge(g["mx_h"], hn + 1)
                STT(mx_rest[:], mx_hi[:], t["part_scale"][0:PARTS * ROWS, 2:3], M[0:PARTS * ROWS, 0, 0:P],
                    ALU.mult, ALU.add).then_inc(g["mx_r"], 1)

            def max_parts(b, half):
                hn = 2 * b + half
                dve.wait_ge(g["mx_r"], hn + 1)
                nc.vector.tensor_copy(mx_mid[:], mx_rest[:]).then_inc(g["mx_m"], 1)
                dve.wait_ge(g["mx_m"], hn + 1)
                if hn:
                    dve.wait_ge(g["shift_in"], 16 * PARTS * hn)
                STT(mx_part[:], mx_mid[:], t["part_scale"][0:PARTS * ROWS, 3:4], mx_rest[:], ALU.mult, ALU.add).then_inc(g["mx_done"], 1)

            def values(b, u):
                half, j = divmod(u, KT)
                if j < KT - 1:
                    return
                dve.wait_ge(g["pv_mm"], b * UNITS + u + 1)
                if b:
                    dve.wait_ge(g["o_normed"], b)
                nc.vector.tensor_copy(o_sb[:, half, :], O[:]).then_inc(g["o_copied"], 1)

            def proj(b):
                dve.wait_ge(g["proj_mm"], b + 1)
                STT(x1[:], R[:, 2, :], v["proj_b"], X[:, b, :], ALU.add, ALU.add).then_inc(g["x1_done"], 1)

            def fc2(b):
                dve.wait_ge(g["fc2_mm"], b + 1)
                STT(x2[:], R[:, 2, :], v["fc2_b"], x1[:], ALU.add, ALU.add).then_inc(g["x2_done"], 1)

            def keys(b):
                dve.wait_ge(g["shift_mm"], b + 1)
                if b:
                    dve.wait_ge(g["s1_mm"], STAGES * b)
                nc.vector.tensor_copy(xbd[C:P, 0:PAD, 1], R[C:P, 2, 0:PAD]).then_inc(g["xbd_pad"], 1)

            def round_query(b, h):
                dve.wait_ge(g["z_copied"], b * H1 + h + 1)
                if b and h == 0:
                    dve.wait_ge(g["fin_mm"], b)
                nc.vector.tensor_copy(z16[:, :, h, :], z[:, :, h, :]).then_inc(g["z_cast"], 1)

            def tokens(b, r):
                n = BLOCKS // TOKS
                dve.wait_ge(g["tok_mm"], b * TOKS + r + 1)
                nc.vector.tensor_copy(x_tok[:, r * n:(r + 1) * n, :],
                                      R[:, (2 + r) % 3, :].rearrange("p (k m) -> p k m", m=P)).then_inc(g["tok_copied"], 1)

            def windows(b, r):
                dve.wait_ge(g["sw_mm"], b * STAGES + r + 1)
                TT(s_win[:, r * UPS * 2:(r + 1) * UPS * 2, :], R[:, r % 3, 0:UPS * 2 * GK].rearrange("p (s k) -> p s k", k=GK),
                   t["window_mask"][:].rearrange("p (s k) -> p s k", k=GK), ALU.add).then_inc(g["sw_masked"], 1)

            def win_max(b):
                dve.wait_ge(g["sw_masked"], (b + 1) * STAGES)
                nc.vector.tensor_reduce(neg_m1[:, :, 0, :], s_win.rearrange("p (g s) k -> p g s k", g=GSEL), AX_X, ALU.max,
                                        negate=True).then_inc(g["sw_max"], 1)
                dve.wait_ge(g["sw_max"], b + 1)
                nc.vector.tensor_copy(neg_m1[:, :, 1, :], neg_m1[:, :, 0, :])
                nc.vector.tensor_copy(neg_m1[:, :, 2, :], neg_m1[:, :, 0, :]).then_inc(g["m1_rep"], 1)

            rows1 = slice(0, PARTS * 2 * UPG)

            def win_rows(b):
                dve.wait_ge(g["m1_t"], b + 1)
                ps = R[rows1, 2, 0:GSEL * P].rearrange("p (g n) -> p g n", g=GSEL)
                nc.vector.tensor_copy(m1_hi[:], ps).then_inc(g["m1_h"], 1)
                dve.wait_ge(g["m1_h"], b + 1)
                STT(m1_rest[:], m1_hi[:], t["part_scale"][rows1, 0:1], ps, ALU.mult, ALU.add).then_inc(g["m1_r"], 1)

            def win_parts(b):
                dve.wait_ge(g["m1_r"], b + 1)
                nc.vector.tensor_copy(m1_mid[:], m1_rest[:]).then_inc(g["m1_m"], 1)
                dve.wait_ge(g["m1_m"], b + 1)
                STT(m1_part[:], m1_mid[:], t["part_scale"][rows1, 1:2], m1_rest[:], ALU.mult, ALU.add).then_inc(g["m1_done"], 1)

            def blk_mask(b, r):
                dve.wait_ge(g["p1_exp"], b * STAGES + r + 1)
                TT(p1[:, r % 2, :], p1[:, r % 2, :], t["block_mask"][:], ALU.min).then_inc(g["p1_masked"], 1)

            def blk_out(b, r):
                n = b * STAGES + r
                dve.wait_ge(g["pv1_mm"], n + 1)
                dve.wait_ge(g["rden1_done"], n + 1)
                k = TG // STAGES
                TT(y1[:, :, r * k:(r + 1) * k, :].rearrange("p h t q -> p t h q"),
                   R[:, 2, :].rearrange("p (t h q) -> p t h q", h=H1, q=TQ),
                   rden[:, r % 2, :].rearrange("p (t h q) -> p t h q", h=H1, q=TQ), ALU.mult).then_inc(g["y1_done"], 1)

            def unify(b, h0):
                if h0 + 2 < H1:
                    return
                dve.wait_ge(g["fin_mm"], b + 1)
                STT(x3[:, b, :], R[:, 0, :], v["attn_b"], x2[:], ALU.add, ALU.add).then_inc(g["x3_done"], 1)

            for i in range(2):
                nc.vector.memset(KX[i][KQ:KQ + PARTS, :, :], 1.0).then_inc(g["ones_rows"], 1)
            nc.vector.memset(abd[:], 0.0).then_inc(g["fills"], 1)
            nc.vector.memset(gbd[:], 0.0).then_inc(g["fills"], 1)
            dve.wait_ge(g["x_in"], 32)
            dve.wait_ge(g["consts_in"], 16 * len(CONSTS))
            dve.wait_ge(g["weights_in"], 16 * (len(WEIGHTS) + 1))
            run({"ln_mean": ln_mean, "ln_scale": ln_scale, "project": project, "max_piece": max_piece, "max_neg": max_neg,
                 "max_rows": max_rows, "max_parts": max_parts, "values": values, "proj": proj, "fc2": fc2, "keys": keys,
                 "round_query": round_query, "tokens": tokens, "windows": windows, "win_max": win_max, "win_rows": win_rows, "win_parts": win_parts,
                 "blk_mask": blk_mask, "blk_out": blk_out, "unify": unify})

            dve.wait_ge(g["wx_copied"], B)
            nc.vector.tensor_reduce(stat[:, 4:5], stat[:, 0:4], AX_X, ALU.add).then_inc(g["wsum"], 1)
            dve.wait_ge(g["mean_mm"], 1)
            TS(stat[:, 5:6], R[:, 0, 0:1], -1.0, None, ALU.mult).then_inc(g["mean_done"], 1)
            dve.wait_ge(g["bn_rstd"], 1)
            TT(stat[:, 9:10], stat[:, 8:9], v["gamma"], ALU.mult).then_inc(g["bn_a"], 1)
            dve.wait_ge(g["bn_a"], 1)
            STT(stat[:, 10:11], stat[:, 5:6], stat[:, 9:10], v["beta"], ALU.mult, ALU.add).then_inc(g["bn_b"], 1)
            dve.wait_ge(g["bn_b"], 1)
            flat = wx[:].rearrange("p s b c -> p (s b c)")
            TS(flat, flat, stat[:, 9:10], stat[:, 10:11], ALU.mult, ALU.add).then_inc(g["bn_done"], 1)

            def new_starts(dst, ends, last_sem):
                nc.vector.tensor_copy(dst[:, :, 1:CH], ys[:, L - 1, :, 0:CH - 1])
                nc.vector.tensor_copy(dst[:, :, 0], R[:, 0, 0:B]).then_inc(last_sem, 1)

            dve.wait_ge(g["gram_mm"], 1)
            nc.vector.tensor_reduce(stat[:, 11:12], R[:, 2, 0:P], AX_X, ALU.add, apply_absolute_value=True).then_inc(g["gram_sum"], 1)
            dve.wait_ge(g["gram_sum"], 1)
            TS(stat[:, 14:15], stat[:, 11:12], 1.0 / GRAM_LIMIT, None, ALU.mult).then_inc(g["gram_share"], 1)
            dve.wait_ge(g["ends_mm"], 1)
            new_starts(y0, None, g["y0_done"])
            dve.wait_ge(g["ends_mm"], 2)
            new_starts(y0n, None, g["y0_moved"])
            dve.wait_ge(g["y0_moved"], 1)
            TT(ydiff[:], y0n[:], y0[:], ALU.subtract).then_inc(g["ydiff_a"], 1)
            dve.wait_ge(g["ydiff_a"], 1)
            nc.vector.tensor_reduce(stat[:, 15:16], ydiff[:].rearrange("p b c -> p (b c)"), AX_X, ALU.max,
                                    apply_absolute_value=True).then_inc(g["ydiff_m"], 1)
            dve.wait_ge(g["ydiff_m"], 1)
            STT(stat[:, 12:13], stat[:, 15:16], 1.0 / START_TOL, stat[:, 14:15], ALU.mult, ALU.max).then_inc(g["ydiff_b"], 1)
            dve.wait_ge(g["dmax_t"], 1)
            nc.vector.tensor_reduce(stat[0:1, 13:14], R[0:1, 1, 0:P], AX_X, ALU.max).then_inc(g["flag_a"], 1)
            dve.wait_ge(g["flag_a"], 1)
            TS(flag[0:1, 0:1], stat[0:1, 13:14], 1.0, None, ALU.is_gt)
            nc.vector.tensor_copy(y0[:], y0n[:]).then_inc(g["flag_b"], 1)
            dve.wait_ge(g["flag_b"], 1)
            moved = dve.value_load(flag[0:1, 0:1])
            with dve.If(moved):
                with dve.Fori(0, ALL_PASSES) as i:
                    dve.wait_ge(g["xends_mm"], i + 1)
                    new_starts(y0, None, g["xy0_done"])
            TT(res[:].rearrange("p b (c s) -> p b c s", s=L), ys[:].rearrange("p s b c -> p b c s"),
               x3[:].rearrange("p b (c s) -> p b c s", s=L), ALU.add).then_inc(g["res_done"], 1)


_PLAIN = ["x"] + CONSTS + WEIGHTS + ["vectors"]


def kernel(**inputs):
    import numpy as np
    import concourse.bacc as bacc
    from concourse.bass_utils import run_bass_kernel_spmd

    f = np.float32
    g = {k: np.asarray(x) for k, x in inputs.items()}

    def both(m):
        o = np.zeros((2 * m.shape[0], 2 * m.shape[1]), m.dtype)
        o[:m.shape[0], :m.shape[1]] = m
        o[m.shape[0]:, m.shape[1]:] = m
        return o

    def twice(x):
        return np.concatenate([x, x])

    pp = np.arange(P)
    arr = {"ident": np.eye(P, dtype=f)}
    arr["mean_c"] = both(np.full((C, C), 1.0 / C, f))
    arr["mean_all"] = (pp[:, None] % C == pp[None] % C).astype(f) / f(B * N)
    arr["shift_half"] = (pp[:, None] + C == pp[None]).astype(f)
    arr["den_select"] = (pp[:, None] == pp[None] // HP * HP + HD).astype(f)
    q, k = (pp % (H1 * TQ)) % TQ, np.arange(GK)
    ok = (k[None] >= q[:, None]) & (k[None] - q[:, None] < W)
    arr["window_mask"] = np.tile(np.where(ok, 0.0, -1e30).astype(f), (1, 2 * UPS))
    col = np.arange(BQ)
    q = col // (H1 * TQ) * TQ + col % TQ
    ok = (pp[:, None] // 2 >= q[None]) & (pp[:, None] // 2 - q[None] < W)
    arr["block_mask"] = np.tile(np.where(ok, 1e30, 0.0).astype(f), (1, BPS))
    row = np.arange(PARTS * 2 * UPG)
    unit, half = row % (2 * UPG) // 2, row % 2
    arr["unit_select"] = ((unit[:, None, None] == np.arange(UPG)[None, :, None])
                          & (half[:, None, None] == (pp % 2)[None, None])).astype(f)
    arr["block_ones"] = (pp[:, None] % 2 == pp[None] // C).astype(f)
    arr["part_scale"] = np.stack([-(pp >= r).astype(f) for r in (2 * UPG, 4 * UPG, ROWS, 2 * ROWS)], 1)

    arr["x"] = np.ascontiguousarray(g["x"].reshape(B, C, N))
    wqkv = g["L0_conv_qkv_w"]
    arr["wq"], arr["wk"], arr["wv"] = (both(wqkv[i * C:(i + 1) * C].T) for i in range(3))
    wp = np.zeros((P, C), f)
    for h in range(H0):
        wp[h * HP:h * HP + HD] = g["L0_conv_proj_w"].T[h * HD:(h + 1) * HD]
    arr["wproj"] = wp
    w1 = np.zeros((P, 2, P), f)
    for half in range(2):
        w1[half * C:(half + 1) * C, half] = g["L0_conv_fc1_w"].T
    arr["wfc1"] = w1
    arr["wfc2"] = np.ascontiguousarray(g["L0_conv_fc2_w"].T)

    def padded(m):
        return np.concatenate([m, np.zeros_like(m)])
    for n, w in (("w1q", "L1_attn_Wq"), ("w1k", "L1_attn_Wk"), ("w1v", "L1_attn_Wv")):
        arr[n] = padded(np.ascontiguousarray(g[w].reshape(H1, C, C).transpose(1, 0, 2)))
    arr["w1u"] = padded(np.ascontiguousarray(g["L1_attn_Wu"].T.reshape(H1, C, C).transpose(1, 0, 2)))
    arr["w_in"] = both(g["L1_ffn_W"].T)
    arr["v_rec"] = both(g["L1_ffn_V"].T)
    vecs = {"ln1_w": "L0_conv_ln1_w", "ln1_b": "L0_conv_ln1_b", "proj_b": "L0_conv_proj_b", "ln2_w": "L0_conv_ln2_w",
            "ln2_b": "L0_conv_ln2_b", "fc2_b": "L0_conv_fc2_b", "attn_b": "L1_attn_bu", "gamma": "L1_ffn_gamma",
            "beta": "L1_ffn_beta"}
    arr["vectors"] = np.stack([g["L0_conv_fc1_b"] if n == "fc1_b" else twice(g[vecs[n]]) for n in VECTORS], 1)

    nc = bacc.Bacc("TRN2", target_bir_lowering=False, num_devices=1)
    arrays, aps = {}, {}
    for n in _PLAIN:
        arrays[n] = np.ascontiguousarray(arr[n])
        aps[n] = nc.dram_tensor(n, arrays[n].shape, mybir.dt.from_np(arrays[n].dtype), kind="ExternalInput").ap()
    out = nc.dram_tensor("result", (B, C, N), F32, kind="ExternalOutput").ap()
    build(nc, aps, out)
    r = run_bass_kernel_spmd(nc, [arrays], core_ids=[0])
    return r.results[0]["result"].reshape(B, C, 32, 32)
```

```python
from contextlib import ExitStack

import concourse.bass as bass
from concourse import mybir

F32 = mybir.dt.float32
BF16 = mybir.dt.bfloat16
I32 = mybir.dt.int32
ALU = mybir.AluOpType
ACT = mybir.ActivationFunctionType
AX_X = mybir.AxisListType.X

P = 128
B, C, N = 4, 64, 1024
HALF = N // 2
H0 = 4
HD = C // H0
HP = P // H0
KT = N // P
PARTS = 3
RUNS = (((0, 2), (1, 1), (2, 0)), ((0, 1), (1, 0)), ((0, 0),))
TERMS = sum(len(r) for r in RUNS)
KQ = TERMS * HD
QT = KT // 2
ROWS = H0 * QT
PIECES = ROWS * 2
UNITS = KT * 2

H1 = 8
W = 32
TQ = 4
TG = HALF // TQ
NG = P // (H1 * TQ)
GU = TG // NG
GK = W + TQ
BLOCKS = HALF // W
BK = 2 * W
BQ = H1 * W
PAD = W - 1
XW = HALF + W
WX_PARTS = B + 1
STAGES = 8
TOKS = 4
BPS = BLOCKS // STAGES
UPS = GU // STAGES
RC = HALF // STAGES
GSEL = 2
UPG = GU // GSEL

L = 8
CH = HALF // L
RUNNERS = 2
BR = B // RUNNERS
COLS = BR * CH
FIRSTS = (6, 0, 0)
WARM = sum(L - first for first in FIRSTS[:-1])
ALL_PASSES = 2 * CH
START_TOL = 2.0 ** -18
GRAM_LIMIT = 4.0

VECTORS = ["ln1_w", "ln1_b", "proj_b", "ln2_w", "ln2_b", "fc1_b", "fc2_b", "attn_b", "gamma", "beta"]
FIRST = {"mean_c": P, "vectors": len(VECTORS), "wq": P, "wk": P, "wv": P}
REST = {"ident": P, "mean_all": P, "shift_half": P, "den_select": P, "window_mask": 2 * UPS * GK, "block_mask": BPS * BQ,
        "block_ones": P, "part_scale": 4, "wproj": C, "wfc1": 2 * P, "wfc2": C, "w_in": P, "v_rec": P}
EARLY = {"w1q": H1 * C, "w1k": H1 * C, "w1v": H1 * C, "w1u": H1 * C, "unit_select": UPG * P}


def layernorm_stages(b, which, i=0):
    return [(n, b, which, i) for n in ("ln_mean", "ln_square", "ln_var", "ln_scale")]


def project_stages(b):
    return [*layernorm_stages(b, 1), ("project", b), ("split", b)]


def max_stages(b, half, units, done=0):
    pieces = [("max_piece", b, half, i) for i in range(done, PIECES)]
    per = -(-len(pieces) // (units - 1))
    out = [pieces[i * per:(i + 1) * per] for i in range(units - 1)]
    return out + [[("max_neg", b, half), ("max_rows", b, half), ("max_parts", b, half)]]


def mlp_stages(b):
    return [("den", b), ("den_exp", b), ("o_norm", b, 0), ("o_norm", b, 1), ("proj", b), *layernorm_stages(b, 2), ("fc1", b), ("fc2", b)]


def merged(main, other, start=0):
    room = [ROOM.get(name, 1.0) for name, *_ in other]
    cost = [0.0 if i < start else COST.get(name, 1.0) for i, (name, *_) in enumerate(main)]
    out, done, total, through = [], 0, 0.0, 0.0
    for x, c in zip(main, cost):
        out.append(x)
        through += c
        while done < len(other) and total + room[done] <= sum(room) * through / sum(cost) + 1e-6:
            if not through:
                break
            total += room[done]
            out.append(other[done])
            done += 1
    return out + other[done:]


UNIFY_CUT = 5
MAX_UNITS = 7
VALUES_AFTER = 4
MAX_EARLY = 4
FIRST_GAP = 3
COST = {"scores": 1.15, "values": 1.12, "max_piece": 0.59}


def unify_parts(b):
    return 2 if b == B - 1 else 1


def out_stages(b, i):
    return [*layernorm_stages(b, 4, i), ("wx", b, i)]


def window_stages(b):
    out = [("keys", b), ("round", b)]
    for h in range(H1):
        out.append(("queries", b, h))
        if h:
            out.append(("round_query", b, h - 1))
    out += [("tokens", b, 0), ("round_query", b, H1 - 1)] + [("tokens", b, r) for r in range(1, TOKS)]
    for r in range(STAGES):
        out.append(("windows", b, r))
        if r == STAGES // GSEL:
            out.append(("win_max", b, 0))
    out += [("win_max", b, 1), ("win_rows", b), ("win_parts", b), ("blk_scores", b, 0), ("blk_mask", b, 0)]
    for r in range(STAGES):
        if r + 1 < STAGES:
            out.append(("blk_scores", b, r + 1))
        out.append(("blk_den", b, r))
        if r + 1 < STAGES:
            out.append(("blk_mask", b, r + 1))
        out.append(("blk_out", b, r))
    unify = [[("unify", b, h, i) for h in range(0, H1, 2)] for i in range(unify_parts(b))]
    if len(unify) > 1:
        at = out.index(("blk_out", b, UNIFY_CUT)) + 1
        first = unify[0] + out_stages(b, 0)
        out[at:] = merged(out[at:], first)
    return out + unify[-1]


def rest_stages(b):
    return [*mlp_stages(b), *layernorm_stages(b, 3), *window_stages(b), *out_stages(b, 0)]


def attend_stages(b):
    out = []
    for half in range(2):
        if half == 0:
            ahead = max_stages(b, 1, MAX_UNITS, 0 if b else MAX_EARLY)
        else:
            ahead = max_stages(b + 1, 0, MAX_UNITS) if b + 1 < B else []
        ahead += [[]] * (KT - len(ahead))
        for j in range(KT):
            u = half * KT + j
            pieces = ahead[j]
            for h in range(H0):
                out += [("scores", b, u, h), *pieces[len(pieces) * h // H0:len(pieces) * (h + 1) // H0]]
                if u and h + 1 == VALUES_AFTER:
                    out.append(("values", b, u - 1))
    return out + [("values", b, UNITS - 1)]


ROOM = {"ln_mean": 2.52, "ln_square": 1.1, "ln_var": 2.94, "ln_scale": 1.52, "den": 3.0, "den_exp": 0.81,
        "o_norm": 2.52, "proj": 2.21, "fc1": 4.2, "fc2": 4.3, "keys": 2.82, "round": 1.96, "round_query": 1.01,
        "queries": 1.0, "tokens": 0.32, "windows": 0.7, "win_max": 2.43, "win_rows": 1.22, "win_parts": 6.02,
        "blk_scores": 1.53, "blk_mask": 0, "blk_den": 1.4, "blk_out": 0.74, "unify": 0.49, "wx": 1.78}

LAST_CUT = 2


def order_of_stages():
    out = [*project_stages(0), ("products",), *project_stages(1), *(x for unit in max_stages(0, 0, 2) for x in unit),
           *(("max_piece", 0, 1, i) for i in range(MAX_EARLY))]
    for b in range(B):
        main = attend_stages(b)
        first = project_stages(b + 1) if 0 < b < B - 1 else []
        other = rest_stages(b - 1) if b else []
        start = FIRST_GAP * len(first)
        if first:
            main[:start] = [y for i, x in enumerate(main[:start])
                            for y in ([x, first[i // FIRST_GAP]] if i % FIRST_GAP == FIRST_GAP - 1 else [x])]
            start += len(first)
        if b + 1 == B:
            cut = other.index(("blk_scores", b - 1, LAST_CUT))
            end = other.index(("ln_mean", b - 1, 4, 0))
            other, late, norm = other[:cut], other[cut:end], other[end:end + 4]
        out += merged(main, other, start)
    early = mlp_stages(B - 1)
    out += merged(late, early)
    for x, y in zip(norm, layernorm_stages(B - 1, 3)):
        out += [x, y]
    return out + [("wx", B - 2, 0), *window_stages(B - 1), *out_stages(B - 1, 1)]


def build(nc, a, out):
    with ExitStack() as ctx:
        def sb(name, shape, dt=F32):
            return ctx.enter_context(nc.sbuf_tensor(name, shape, dt))

        def sem(name):
            return ctx.enter_context(nc.semaphore(name))

        pack = {n: sb("s_" + n, [P, sum(cols.values())]) for n, cols in (("first", FIRST), ("rest", REST))}
        zs = sb("zs", [P, GU * 2 * GK + TG * H1 * TQ // 2])
        pack["early"] = zs[:, 0:sum(EARLY.values())]
        t = {}
        for which, cols in (("first", FIRST), ("rest", REST), ("early", EARLY)):
            at = 0
            for n, width in cols.items():
                t[n] = pack[which][:, at:at + width]
                at += width
        v = {n: t["vectors"][:, i:i + 1] for i, n in enumerate(VECTORS)}
        for n in ("w1q", "w1k", "w1v", "w1u"):
            t[n] = t[n].rearrange("p (h m) -> p h m", h=H1)
        t["wfc1"] = t["wfc1"].rearrange("p (a m) -> p a m", a=2)
        t["unit_select"] = t["unit_select"][0:PARTS * 2 * UPG, :].rearrange("p (u m) -> p u m", u=UPG)
        eps = sb("eps", [P, 1])
        unit_sel = sb("unit_sel", [PARTS * 2 * UPG, UPG, P], BF16)
        abd = sb("abd", [P, H1, P])
        gbd = sb("gbd", [P, H1, P])
        zeros16 = abd[:, :, :].rearrange("p h m -> p (h m)").bitcast(BF16)
        ones16 = unit_sel[:, :, :].rearrange("p u m -> p (u m)")

        X = sb("X", [P, B, HALF])
        ln_d = sb("ln_d", [P, HALF])
        ln_q = sb("ln_q", [P, HALF])
        ln_l = sb("ln_l", [P, HALF])
        ln_r = sb("ln_r", [P, HALF])
        x_ln = sb("x_ln", [P, HALF])
        qk_part = sb("qk_part", [P, 2, PARTS, HALF], BF16)
        qk_rows = qk_part[:, :, :, :].rearrange("p q r n -> p (q r) n")
        hi_rows = qk_rows[:, 0:2 * PARTS:2 * PARTS - 1, :]
        mid_rows = qk_rows[:, 1:2 * PARTS - 1:2 * PARTS - 3, :]
        qk_rest = sb("qk_rest", [P, 2, HALF])
        QX_all = [sb(f"QX{i}", [P, 2, H0, HALF], BF16) for i in range(2)]
        KX_all = [sb(f"KX{i}", [P, 2, H0, HALF], BF16) for i in range(2)]
        QX = [x[0:KQ + PARTS, :, :, :] for x in QX_all]
        KX = [x[0:KQ + PARTS, :, :, :] for x in KX_all]
        VT = [sb(f"VT{i}", [P, KT, H0, HP]) for i in range(2)]
        part_max = sb("part_max", [P, ROWS, 2])
        neg_max = sb("neg_max", [P, PARTS, ROWS])
        mx_hi = sb("mx_hi", [PARTS * ROWS, P], BF16)
        mx_rest = sb("mx_rest", [PARTS * ROWS, P])
        mx_mid = sb("mx_mid", [PARTS * ROWS, P], BF16)
        mx_part = sb("mx_part", [PARTS * ROWS, P], BF16)
        rlog = sb("rlog", [P, 2, HALF])
        probs = sb("probs", [P, 2, H0, HALF])
        o_sb = sb("o_sb", [P, 2, HALF])
        rden = sb("rden", [P, 2, HALF])
        rstep = sb("rstep", [P, 2, HALF])
        o_norm = sb("o_norm", [P, 2, HALF])
        x1 = sb("x1", [P, HALF])
        hid = o_norm
        x2s = [sb(f"x2_{i}", [P, HALF]) for i in range(2)]
        idle = [x[:, :, :, :].rearrange("p a h n -> p (a h n)").bitcast(F32) for x in (QX_all[B % 2], KX_all[B % 2])]
        last_rlog, last_rden = (idle[0][:, i * 2 * HALF:(i + 1) * 2 * HALF].rearrange("p (a n) -> p a n", a=2) for i in range(2))
        last_rstep = idle[1][:, 0:2 * HALF].rearrange("p (a n) -> p a n", a=2)
        last_ln = {n: idle[i // 2][:, i % 2 * HALF + (i // 2) * 2 * HALF:][:, 0:HALF]
                   for i, n in enumerate(("ln_d", "ln_q", "ln_l", "ln_r"))}

        xh = sb("xh", [P, HALF])
        xbd = sb("xbd", [P, XW, 2])
        xbd16 = sb("xbd16", [P, 2, XW], BF16)
        z = sb("z", [P, TG, H1, TQ])
        z16 = zs[:, 0:TG * H1 * TQ // 2].bitcast(BF16).rearrange("p (t h q) -> p t h q", h=H1, q=TQ)
        s_win = zs[:, TG * H1 * TQ // 2:].rearrange("p (s k) -> p s k", k=GK)
        y1 = zs[:, 0:H1 * TG * TQ].rearrange("p (h t q) -> p h t q", h=H1, q=TQ)
        x_tok = sb("x_tok", [P, BLOCKS, P])
        neg_m1 = sb("neg_m1", [P, GSEL, PARTS, 2 * UPG])
        m1_hi = sb("m1_hi", [PARTS * 2 * UPG, GSEL, P], BF16)
        m1_rest = sb("m1_rest", [PARTS * 2 * UPG, GSEL, P])
        m1_mid = sb("m1_mid", [PARTS * 2 * UPG, GSEL, P], BF16)
        m1_part = sb("m1_part", [PARTS * 2 * UPG, GSEL, P], BF16)
        p1 = sb("p1", [P, 2, BPS * BQ])
        x3 = sb("x3", [P, B, HALF])

        wx = sb("wx", [P, L, B, CH])
        ys = probs[:, 0, :, :].rearrange("p a n -> p (a n)").rearrange("p (s b c) -> p s b c", s=L, b=B)
        y0 = sb("y0", [P, B, CH])
        y0n, ydiff = (x[:, 0:B * CH].rearrange("p (b c) -> p b c", b=B) for x in (ln_q, ln_l))
        stat = sb("stat", [P, 16])
        bn_parts = sb("bn_parts", [P, WX_PARTS, 6])
        flag = sb("flag", [1, 2], I32)
        res = probs[:, 1, :, :]

        S = ctx.enter_context(nc.psum_tensor("S", [P, 2, 512], F32))
        O = ctx.enter_context(nc.psum_tensor("O", [P, 512], F32))
        R = ctx.enter_context(nc.psum_tensor("R", [P, 3, 512], F32))
        M = ctx.enter_context(nc.psum_tensor("M", [P, 2, 512], F32))

        scratch = nc.dram_tensor("qk_scratch", [B, 2, 2, PARTS, HD, H0, HALF], BF16, kind="Internal").ap()

        names = """x0_in first_in x_in rest_in early_in fills pool_fills unit_sel_done abd_mm gbd_mm abd_done
            ln_mean ln_ctr ln_sq ln_var ln_log ln_rstd ln_norm ln_out
            qk_mm v_mm qk_hi qk_rst qk_mid qk_lo qk_dram qk_in v_copied
            max_mm max_red negmax negmax_t mx_h mx_r mx_m mx_done shift_in
            st_mm exp_done pv_mm o_copied den_mm den_log rden_done den_prod rden_new o_normed proj_mm x1_done
            fc1_mm gelu_done fc2_mm x2_done
            shift_mm xbd_a xbd_pad xbd_cast z_mm z_copied z_cast tok_mm tok_copied
            sw_mm sw_masked sw_max m1_rep m1_t m1_h m1_r m1_m m1_done
            s1_mm p1_exp p1_masked den1_mm den1_log rden1_done pv1_mm y1_done fin_mm x3_done
            wx_mm wx_copied bn_part bn_own bn_mm bn_mean bn_shift bn_sq bn_var bn_log bn_rstd bn_a bn_b bn_done
            gram_mm gram_sum gram_share ydiff_m pre_mm y_done ends_mm y0_moved y0_done ydiff_a ydiff_b
            dmax_t flag_a flag_b xpre_mm xy_done xends_mm xy0_done res_done xres_done out_done""".split()
        g = {n: sem(n) for n in names}

        def half_rows(h):
            return slice(h * C, (h + 1) * C)

        timeline = order_of_stages()
        lns = [a for name, *a in timeline if name == "ln_mean"]
        affine = [a for a in lns if a[1] in (1, 2)]

        def ln_no(b, which, i=0):
            return lns.index([b, which, i])

        def ln_cols(b, which, i):
            r0, r1 = unify_rounds(b, i) if which == 4 else (0, STAGES)
            return slice(r0 * RC, r1 * RC)

        def ln_in(b, which, i):
            return {1: X[:, b, :], 2: x1[:, :], 3: x2s[b % 2][:, :], 4: x3[:, b, :]}[which][:, ln_cols(b, which, i)]

        def apart(b, which=2):
            return b == B - 1 and which in (2, 3)

        def ln_bufs(b, which, i=0):
            return {n: x[:, ln_cols(b, which, i)] for n, x in (last_ln if apart(b, which) else own_ln).items()}

        def ln_bank(b, which, i, k):
            if apart(b, which):
                bank = M[:, k, :]
            elif which == 4 and i + 1 < unify_parts(b):
                bank = O[:, :]
            else:
                bank = R[:, k + (which == 4), :]
            return bank[:, ln_cols(b, which, i)]

        def chunks(b, i):
            c = ln_cols(b, 4, i)
            return slice(c.start // L, c.stop // L)

        def wx_bank(b, i):
            return (O[:, :] if i + 1 < unify_parts(b) else R[:, 0, :])[:, ln_cols(b, 4, i)]

        def ln_dst(b, which, i=0):
            return ln_bufs(b, which, i)["ln_d"] if which < 3 or (b, which) == (B - 2, 4) else xh[:, ln_cols(b, which, i)]

        def pair(b):
            return M[:, 0:2, :] if apart(b) else R[:, 0:2, :]

        def single(b):
            return S[:, 0, :] if apart(b) else R[:, 2, :]

        def recip_bufs(b):
            return (last_rlog, last_rden, last_rstep) if apart(b) else (rlog[:, :, :], rden[:, :, :], rstep[:, :, :])

        def unify_rounds(b, i):
            return (0, STAGES) if unify_parts(b) == 1 else ((0, UNIFY_CUT), (UNIFY_CUT, STAGES))[i]

        def max_ring(n):
            if n < PIECES:
                return [M[:, 0, :], M[:, 1, :], S[:, 0, :], S[:, 1, :]]
            return [M[:, 0, :], M[:, 1, :]] + ([R[:, 1, :], R[:, 2, :]] if n < 3 * PIECES else [])

        def s_ring(n):
            if n >= (B * UNITS - KT) * H0:
                return [M[:, 0, :], M[:, 1, :], S[:, 0, :], S[:, 1, :]]
            return [S[:, 0, :], S[:, 1, :]] + ([R[:, 0, :]] if n < UNITS * H0 else [])

        def unify_bank(b, i):
            return O[:, :] if i + 1 < unify_parts(b) else R[:, 0, :]

        def s1_bank(b, r):
            return S[:, r % 2, :] if b == B - 1 else R[:, 0, :]

        def den1_bank(b, r):
            return M[:, r % 2, :] if b == B - 1 else R[:, 1, :]

        def pv1_bank(b, r):
            return R[:, 1 + r % 2, :] if b == B - 1 else R[:, 2, :]

        def rnn_bank(step, i):
            return (M, S)[i][:, step % 2, 0:COLS].rearrange("p (b c) -> p b c", b=BR)

        own_ln = {"ln_d": ln_d[:, :], "ln_q": ln_q[:, :], "ln_l": ln_l[:, :], "ln_r": ln_r[:, :]}

        def run(stages):
            for name, *args in timeline:
                if name in stages:
                    stages[name](*args)

        block = ctx.enter_context(nc.Block())

        @block.sync
        def _(sp):
            def load_x(b0, b1, signal):
                for half in range(2):
                    sp.dma_start(X[half_rows(half), b0:b1, :],
                                 a["x"][b0:b1, :, half * HALF:(half + 1) * HALF].rearrange("b c n -> c b n")).then_inc(g[signal], 16)

            load_x(0, 1, "x0_in")
            sp.dma_start(pack["first"][:], a["first"]).then_inc(g["first_in"], 16)
            sp.dma_start(pack["early"], a["early"]).then_inc(g["early_in"], 16)
            sp.dma_start(pack["rest"][:], a["rest"]).then_inc(g["rest_in"], 16)
            load_x(1, B, "x_in")

            def relayout(b):
                sp.wait_ge(g["qk_lo"], b + 1)
                for half in range(2):
                    sp.dma_start(scratch[b, half].rearrange("q r d h n -> (d h) (q r) n"),
                                 qk_rows[half_rows(half), :, :]).then_inc(g["qk_dram"], 16)
                sp.wait_ge(g["qk_dram"], 32 * (b + 1))
                if b >= 2:
                    sp.wait_ge(g["st_mm"], H0 * UNITS * (b - 1))
                row = 0
                for run_ in RUNS:
                    rows = len(run_) * HD
                    for q, dst in enumerate((QX[b % 2], KX[b % 2])):
                        p0 = run_[0][0] if q == 0 else PARTS - 1 - run_[0][1]
                        sp.dma_start(dst[row:row + rows, :, :, :].rearrange("p a h n -> p a (h n)"),
                                     scratch[b, :, q, p0:p0 + len(run_)].rearrange("a r d h n -> (r d) a (h n)")
                                     ).then_inc(g["qk_in"], 16)
                    row += rows

            def shift_rows(b, half):
                sp.wait_ge(g["mx_done"], 2 * b + half + 1)
                for p in range(PARTS):
                    sp.dma_start(QX[b % 2][KQ + p:KQ + p + 1, half, :, :].rearrange("o h (t n) -> o (h t) n", n=P),
                                 mx_part[p * ROWS:(p + 1) * ROWS, :]).then_inc(g["shift_in"], 16)

            run({"split": relayout, "max_parts": shift_rows})

            def store():
                for half in range(2):
                    sp.dma_start(out[:, :, half * HALF:(half + 1) * HALF].rearrange("b c n -> c b n"),
                                 res[half_rows(half), :, :]).then_inc(g["out_done"], 16)

            sp.wait_ge(g["res_done"], 1)
            store()
            sp.wait_ge(g["out_done"], 32)
            sp.wait_ge(g["flag_b"], 1)
            moved = sp.value_load(flag[0:1, 0:1])
            with sp.If(moved):
                sp.wait_ge(g["xres_done"], 1)
                store()
                sp.wait_ge(g["out_done"], 64)

        @block.gpsimd
        def _(pool):
            nc.gpsimd.memset(eps[:], 1e-5).then_inc(g["pool_fills"], 1)
            for i in range(2):
                nc.gpsimd.memset(VT[i][:], 0.0).then_inc(g["pool_fills"], 1)
            pool.wait_ge(g["pool_fills"], 3)
            for i in range(2):
                nc.gpsimd.memset(VT[i][:, :, :, HD:HD + 1], 1.0).then_inc(g["pool_fills"], 1)
            nc.gpsimd.memset(xbd[:], 0.0)
            nc.gpsimd.memset(y0[:], 0.5).then_inc(g["pool_fills"], 1)
            for i in range(2):
                pool.wait_ge(g["pool_fills"], 6 + i)
                nc.gpsimd.memset(KX[i][KQ:KQ + PARTS, :, :, :], 1.0).then_inc(g["pool_fills"], 1)

        @block.tensor
        def _(pe):
            mm = nc.tensor.matmul

            def keep_clock(n, src=zeros16):
                for _ in range(n):
                    mm(S[:, 1, :], src[:, 0:P], src[:, 0:512], start=True, stop=True)

            def ln_mean(b, which, i):
                if which == 1 and b >= 3:
                    pe.wait_ge(g["wx_copied"], b - 2)
                elif which == 1 and b:
                    pe.wait_ge(g["qk_rst"], 2 * b)
                    pe.wait_ge(g["x_in"], 32)
                    if b == 1:
                        pe.wait_ge(g["unit_sel_done"], 1)
                elif which == 2:
                    pe.wait_ge(g["x1_done"], b + 1)
                elif which == 3:
                    pe.wait_ge(g["x2_done"], b + 1)
                elif which == 4:
                    pe.wait_ge(g["x3_done"], b + 1 + i)
                mm(ln_bank(b, which, i, 0), t["mean_c"], ln_in(b, which, i), start=True, stop=True).then_inc(g["ln_mean"], 1)

            def ln_var(b, which, i):
                if which == 1 and b < 2:
                    keep_clock(5, ones16 if b else zeros16)
                if b == B - 1 and which in (3, 4) and i + 1 == (unify_parts(b) if which == 4 else 1):
                    keep_clock(5, ones16)
                pe.wait_ge(g["ln_sq"], ln_no(b, which, i) + 1)
                mm(ln_bank(b, which, i, 1), t["mean_c"], ln_bufs(b, which, i)["ln_q"], start=True, stop=True).then_inc(g["ln_var"], 1)

            def project(b):
                if b < 2:
                    keep_clock(8, ones16 if b else zeros16)
                pe.wait_ge(g["ln_out"], affine.index([b, 1, 0]) + 1)
                mm(R[:, 0, :], t["wq"], x_ln[:], start=True, stop=True).then_inc(g["qk_mm"], 1)
                mm(R[:, 1, :], t["wk"], x_ln[:], start=True, stop=True).then_inc(g["qk_mm"], 1)
                if b == 1:
                    pe.wait_ge(g["v_copied"], 1)
                for j in range(QT):
                    last = mm(R[:, 2, j * P:(j + 1) * P], x_ln[:, j * P:(j + 1) * P], t["wv"], start=True, stop=True)
                last.then_inc(g["v_mm"], 1)

            def max_piece(b, half, i):
                h, rest = divmod(i, QT * 2)
                nt, kh = divmod(rest, 2)
                hn = 2 * b + half
                n = hn * PIECES + i
                if i == 0:
                    pe.wait_ge(g["qk_in"], 16 * 2 * len(RUNS) * (b + 1))
                    if hn:
                        pe.wait_ge(g["mx_r"], hn)
                    if hn == 1:
                        pe.wait_ge(g["v_copied"], 2)
                        pe.wait_ge(g["qk_rst"], 4)
                ring = len(max_ring(n))
                if n >= ring:
                    pe.wait_ge(g["max_red"], n - ring + 1)
                mm(max_ring(n)[n % ring], QX[b % 2][0:KQ, half, h, nt * P:(nt + 1) * P], KX[b % 2][0:KQ, kh, h, :],
                   start=True, stop=True).then_inc(g["max_mm"], 1)

            def max_rows(b, half):
                pe.wait_ge(g["negmax"], 2 * b + half + 1)
                mm(M[0:PARTS * ROWS, 0, 0:P], neg_max[:], t["ident"], start=True, stop=True).then_inc(g["negmax_t"], 1)

            def scores(b, u, h):
                half, j = divmod(u, KT)
                n = (b * UNITS + u) * H0 + h
                if j == 0 and h == 0:
                    pe.wait_ge(g["shift_in"], 16 * PARTS * (2 * b + half + 1))
                if n == 0:
                    pe.wait_ge(g["qk_rst"], 4)
                ring = s_ring(n)
                if n >= len(ring):
                    pe.wait_ge(g["exp_done"], n - len(ring) + 1)
                mm(ring[n % len(ring)], KX[b % 2][:, j // QT, h, j % QT * P:(j % QT + 1) * P], QX[b % 2][:, half, h, :],
                   start=True, stop=True).then_inc(g["st_mm"], 1)

            def values(b, u):
                half, j = divmod(u, KT)
                n = b * UNITS + u
                if u == 0:
                    pe.wait_ge(g["v_copied"], b + 1)
                if j == 0 and n:
                    pe.wait_ge(g["o_copied"], 2 * b + half)
                pe.wait_ge(g["exp_done"], H0 * (n + 1))
                for h in range(H0):
                    last = mm(O[h * HP:(h + 1) * HP, :], VT[b % 2][:, j, h, :], probs[:, u % 2, h, :],
                              start=(j == 0), stop=(j == KT - 1))
                last.then_inc(g["pv_mm"], 1)

            def den(b):
                pe.wait_ge(g["o_copied"], 2 * (b + 1))
                if b + 2 < B:
                    pe.wait_ge(g["qk_rst"], 2 * (b + 3))
                elif not apart(b):
                    pe.wait_ge(g["wx_copied"], b)
                else:
                    pe.wait_ge(g["mx_r"], 2 * B)
                for half in range(2):
                    last = mm(pair(b)[:, half, :], t["den_select"], o_sb[:, half, :], start=True, stop=True)
                last.then_inc(g["den_mm"], 1)

            def proj(b):
                if b + 2 < B:
                    pe.wait_ge(g["v_copied"], b + 3)
                for half in range(2):
                    pe.wait_ge(g["o_normed"], 2 * b + half + 1)
                    last = mm(single(b)[half_rows(half), :], t["wproj"], o_norm[:, half, :], start=True, stop=True)
                last.then_inc(g["proj_mm"], 1)

            def fc1(b):
                pe.wait_ge(g["ln_out"], affine.index([b, 2, 0]) + 1)
                for half in range(2):
                    last = mm(pair(b)[:, half, :], t["wfc1"][:, half, :], x_ln[:], start=True, stop=True)
                last.then_inc(g["fc1_mm"], 1)

            def fc2(b):
                pe.wait_ge(g["gelu_done"], b + 1)
                for half in range(2):
                    last = mm(single(b)[half_rows(half), :], t["wfc2"], hid[:, half, :], start=True, stop=True)
                last.then_inc(g["fc2_mm"], 1)

            def keys(b):
                if b == B - 1:
                    keep_clock(3, ones16)
                pe.wait_ge(g["ln_norm"], ln_no(b, 3) + 1)
                mm(R[:, 2, 0:PAD], t["shift_half"], xh[:, HALF - PAD:HALF], start=True, stop=True).then_inc(g["shift_mm"], 1)

            def queries(b, h):
                if h == 0 and b == B - 1:
                    pe.wait_ge(g["wx_copied"], b)
                if h == 2:
                    pe.wait_ge(g["xbd_pad"], b + 1)
                elif h >= 3:
                    pe.wait_ge(g["z_copied"], b * H1 + h - 2)
                mm(R[:, h % 3, :], abd[:, h, :], xh[:], start=True, stop=True).then_inc(g["z_mm"], 1)

            def tokens(b, r):
                pe.wait_ge(g["z_copied"], b * H1 + min(H1, 6 + r))
                if r == 0:
                    pe.wait_ge(g["xbd_a"], b + 1)
                elif r == 3:
                    pe.wait_ge(g["tok_copied"], b * TOKS + 1)
                for k in range(BLOCKS // TOKS):
                    i = r * (BLOCKS // TOKS) + k
                    last = nc.tensor.transpose(R[:, (2 + r) % 3, k * P:(k + 1) * P],
                                               xbd[:, i * W:i * W + BK, :].rearrange("p k a -> p (k a)"), t["ident"])
                last.then_inc(g["tok_mm"], 1)

            def windows(b, r):
                if r == 0:
                    pe.wait_ge(g["xbd_cast"], b + 1)
                    pe.wait_ge(g["z_cast"], H1 * (b + 1))
                if r < 3:
                    pe.wait_ge(g["tok_copied"], b * TOKS + 2 + r)
                else:
                    pe.wait_ge(g["sw_masked"], b * STAGES + r - 2)
                for k in range(UPS):
                    for gi in range(NG):
                        tg = (r * UPS + k) * NG + gi
                        last = mm(R[gi * 32:(gi + 1) * 32, r % 3, k * 2 * GK:(k + 1) * 2 * GK], z16[:, tg, :, :],
                                  xbd16[:, :, tg * TQ:tg * TQ + GK], start=True, stop=True)
                last.then_inc(g["sw_mm"], 1)

            def win_rows(b):
                if b == B - 1:
                    keep_clock(12, ones16)
                pe.wait_ge(g["m1_rep"], b + 1)
                for gs in range(GSEL):
                    last = mm(R[0:PARTS * 2 * UPG, 2, gs * P:(gs + 1) * P], neg_m1[:, gs, :, :], t["ident"], start=True, stop=True)
                last.then_inc(g["m1_t"], 1)

            def blk_scores(b, r):
                n = b * STAGES + r
                if r == 0:
                    if b == B - 1:
                        keep_clock(7, ones16)
                    pe.wait_ge(g["m1_done"], b + 1)
                elif b + 1 < B:
                    pe.wait_ge(g["p1_exp"], n)
                elif r >= 2:
                    pe.wait_ge(g["p1_exp"], n - 1)
                for k in range(BPS):
                    i = r * BPS + k
                    mm(s1_bank(b, r)[:, k * BQ:(k + 1) * BQ], xbd[:, i * W:i * W + BK, :].rearrange("p k a -> p (k a)"),
                       z[:, i * 8:(i + 1) * 8, :, :], start=True, stop=False)
                    for uu in range(2):
                        u = 2 * i + uu
                        last = mm(s1_bank(b, r)[:, k * BQ + uu * P:k * BQ + (uu + 1) * P], unit_sel[:, u % UPG, :], m1_part[:, u // UPG, :],
                                  start=False, stop=(uu == 1))
                last.then_inc(g["s1_mm"], 1)

            def blk_den(b, r):
                n = b * STAGES + r
                pe.wait_ge(g["p1_masked"], n + 1)
                free = n if b + 1 < B else n - 1 if r >= 2 else 0
                if free:
                    pe.wait_ge(g["den1_log"], free)
                mm(den1_bank(b, r), t["block_ones"], p1[:, r % 2, :], start=True, stop=True).then_inc(g["den1_mm"], 1)
                if free:
                    pe.wait_ge(g["y1_done"], free)
                for k in range(BPS):
                    last = mm(pv1_bank(b, r)[:, k * BQ:(k + 1) * BQ], x_tok[:, r * BPS + k, :], p1[:, r % 2, k * BQ:(k + 1) * BQ],
                              start=True, stop=True)
                last.then_inc(g["pv1_mm"], 1)

            def unify(b, h0, i):
                r0, r1 = unify_rounds(b, i)
                if h0 == 0:
                    pe.wait_ge(g["y1_done"], b * STAGES + r1)
                for h in range(h0, h0 + 2):
                    last = mm(unify_bank(b, i)[:, r0 * RC:r1 * RC], gbd[:, h, :], y1[:, h, r0 * RC // TQ:r1 * RC // TQ, :],
                              start=(h == 0), stop=(h == H1 - 1))
                if h0 + 2 == H1:
                    last.then_inc(g["fin_mm"], 1)

            def wx_(b, i):
                if i == 1:
                    keep_clock(7, ones16)
                pe.wait_ge(g["ln_norm"], ln_no(b, 4, i) + 1)
                mm(wx_bank(b, i), t["w_in"], ln_dst(b, 4, i), start=True, stop=True).then_inc(g["wx_mm"], 1)

            def products():
                pe.wait_ge(g["early_in"], 16)
                pe.wait_ge(g["rest_in"], 16)
                pe.wait_ge(g["pool_fills"], 8)
                for h in range(H1):
                    for half in range(2):
                        last = mm(S[half_rows(half), h // 4, (h % 4) * P + half * C:(h % 4) * P + (half + 1) * C],
                                  t["w1q"][:, h, :], t["w1k"][:, h, :], start=True, stop=True)
                last.then_inc(g["abd_mm"], 1)
                for h in range(H1):
                    for half in range(2):
                        last = mm(M[half_rows(half), h // 4, (h % 4) * P + half * C:(h % 4) * P + (half + 1) * C],
                                  t["w1v"][:, h, :], t["w1u"][:, h, :], start=True, stop=True)
                last.then_inc(g["gbd_mm"], 1)
                pe.wait_ge(g["abd_done"], 4)

            pe.wait_ge(g["fills"], 1)
            keep_clock(7)
            pe.wait_ge(g["x0_in"], 32)
            pe.wait_ge(g["first_in"], 16)
            run({"products": products, "ln_mean": ln_mean, "ln_var": ln_var, "project": project, "max_piece": max_piece, "max_rows": max_rows,
                 "scores": scores, "values": values, "den": den, "proj": proj, "fc1": fc1, "fc2": fc2, "keys": keys,
                 "queries": queries, "tokens": tokens, "windows": windows, "win_rows": win_rows, "blk_scores": blk_scores,
                 "blk_den": blk_den, "unify": unify, "wx": wx_})
            keep_clock(3, ones16)
            pe.wait_ge(g["wx_copied"], WX_PARTS)

            keep_clock(4, ones16)
            pe.wait_ge(g["bn_own"], 1)
            mm(R[:, 0, 0:2], t["mean_all"], stat[:, 0:2], start=True, stop=True).then_inc(g["bn_mm"], 1)
            mm(R[:, 2, 0:P], t["v_rec"], t["v_rec"], start=True, stop=True).then_inc(g["gram_mm"], 1)
            keep_clock(10, ones16)
            pe.wait_ge(g["bn_done"], 1)

            def rnn_step(step, first, i, done, at):
                n = at + (step - first) * RUNNERS + i
                bank = rnn_bank(step, i)
                prev = ys[:, step - 1] if step > first else y0
                mm(bank, t["ident"], wx[:, step, i * BR:(i + 1) * BR, :], start=True, stop=False)
                if step > first:
                    pe.wait_ge(done, n - RUNNERS + 1)
                return mm(bank, t["v_rec"], prev[:, i * BR:(i + 1) * BR, :], start=False, stop=True)

            at = 0
            for ps, first in enumerate(FIRSTS):
                if ps:
                    pe.wait_ge(g["y0_done"], ps)
                if ps == 1:
                    pe.wait_ge(g["bn_done"], 2)
                for step in range(first, L):
                    for i in range(RUNNERS):
                        rnn_step(step, first, i, g["y_done"], at).then_inc(g["pre_mm"], 1)
                at += (L - first) * RUNNERS
                pe.wait_ge(g["y_done"], at)
                mm(R[:, 0, 0:B], t["shift_half"], ys[:, L - 1, :, CH - 1], start=True, stop=True).then_inc(g["ends_mm"], 1)
            pe.wait_ge(g["ydiff_b"], 1)
            mm(R[0:1, 1, 0:P], stat[:, 12:13], t["ident"], start=True, stop=True).then_inc(g["dmax_t"], 1)
            pe.wait_ge(g["flag_b"], 1)
            moved = pe.value_load(flag[0:1, 0:1])
            with pe.If(moved):
                with pe.Fori(0, ALL_PASSES) as i:
                    for step in range(L):
                        for runner in range(RUNNERS):
                            rnn_step(step, 0, runner, g["xy_done"], i * (L * RUNNERS)).then_inc(g["xpre_mm"], 1)
                    pe.wait_ge(g["xy_done"], i * (L * RUNNERS) + L * RUNNERS)
                    mm(R[:, 0, 0:B], t["shift_half"], ys[:, L - 1, :, CH - 1], start=True, stop=True).then_inc(g["xends_mm"], 1)
                    pe.wait_ge(g["xy0_done"], i + 1)

        @block.scalar
        def _(act):
            A = nc.scalar.activation

            def ln_square(b, which, i):
                act.wait_ge(g["ln_ctr"], ln_no(b, which, i) + 1)
                A(ln_bufs(b, which, i)["ln_q"], ln_bufs(b, which, i)["ln_d"], ACT.Square).then_inc(g["ln_sq"], 1)

            def ln_var(b, which, i):
                buf = ln_bufs(b, which, i)
                act.wait_ge(g["ln_var"], ln_no(b, which, i) + 1)
                A(buf["ln_l"], ln_bank(b, which, i, 1), ACT.Ln, bias=eps[:, 0:1]).then_inc(g["ln_log"], 1)
                act.wait_ge(g["ln_log"], ln_no(b, which, i) + 1)
                A(buf["ln_r"], buf["ln_l"], ACT.Exp, scale=-0.5).then_inc(g["ln_rstd"], 1)

            def project(b):
                if b:
                    act.wait_ge(g["qk_dram"], 32 * b)
                for q in range(2):
                    act.wait_ge(g["qk_mm"], 2 * b + q + 1)
                    A(hi_rows[:, q, :], R[:, q, :], ACT.Copy).then_inc(g["qk_hi"], 1)
                act.wait_ge(g["v_mm"], b + 1)
                if b >= 2:
                    act.wait_ge(g["pv_mm"], UNITS * (b - 1))
                for half in range(2):
                    last = A(VT[b % 2][:, half * QT:(half + 1) * QT, :, 0:HD],
                             R[:, 2, :].rearrange("p (j a h d) -> p a j h d", j=QT, a=2, h=H0)[:, half], ACT.Copy)
                last.then_inc(g["v_copied"], 1)

            def scores(b, u, h):
                n = b * UNITS + u
                if n >= 2 and h == 0:
                    act.wait_ge(g["pv_mm"], n - 1)
                act.wait_ge(g["st_mm"], H0 * n + h + 1)
                ring = s_ring(H0 * n + h)
                A(probs[:, u % 2, h, :], ring[(H0 * n + h) % len(ring)], ACT.Exp, scale=HD ** -0.5).then_inc(g["exp_done"], 1)

            def den(b):
                act.wait_ge(g["den_mm"], b + 1)
                A(recip_bufs(b)[0], pair(b), ACT.Ln).then_inc(g["den_log"], 1)

            def den_exp(b):
                act.wait_ge(g["den_log"], b + 1)
                A(recip_bufs(b)[1], recip_bufs(b)[0], ACT.Exp, scale=-1.0).then_inc(g["rden_done"], 1)

            def fc1(b):
                act.wait_ge(g["fc1_mm"], b + 1)
                A(hid[:, :, :], pair(b), ACT.Gelu, bias=v["fc1_b"]).then_inc(g["gelu_done"], 1)
                nc.scalar.preload_act_table_set("natural_log_exp_and_others")

            def queries(b, h):
                act.wait_ge(g["z_mm"], b * H1 + h + 1)
                A(z[:, :, h, :], R[:, h % 3, :].rearrange("p (t q) -> p t q", q=TQ), ACT.Copy).then_inc(g["z_copied"], 1)

            def blk_scores(b, r):
                n = b * STAGES + r
                act.wait_ge(g["s1_mm"], n + 1)
                if n >= 2:
                    act.wait_ge(g["pv1_mm"], n - 1)
                A(p1[:, r % 2, :], s1_bank(b, r), ACT.Exp).then_inc(g["p1_exp"], 1)

            def blk_den(b, r):
                n = b * STAGES + r
                act.wait_ge(g["den1_mm"], n + 1)
                if n >= 2:
                    act.wait_ge(g["y1_done"], n - 1)
                A(rlog[:, r % 2, :], den1_bank(b, r), ACT.Ln).then_inc(g["den1_log"], 1)
                act.wait_ge(g["den1_log"], n + 1)
                A(rden[:, r % 2, :], rlog[:, r % 2, :], ACT.Exp, scale=-1.0).then_inc(g["rden1_done"], 1)

            def wx_(b, i):
                act.wait_ge(g["wx_mm"], b + 1 + i)
                A(wx[:, :, b, chunks(b, i)], wx_bank(b, i).rearrange("p (c s) -> p s c", s=L), ACT.Copy).then_inc(g["wx_copied"], 1)

            def products():
                act.wait_ge(g["abd_mm"], 1)
                act.wait_ge(g["fills"], 2)
                for half in range(2):
                    A(abd[half_rows(half), :, half_rows(half)],
                      S[half_rows(half), :, :].rearrange("p k (h m) -> p (k h) m", h=4)[:, :, half_rows(half)],
                      ACT.Copy, scale=0.125).then_inc(g["abd_done"], 1)
                act.wait_ge(g["gbd_mm"], 1)
                for half in range(2):
                    A(gbd[half_rows(half), :, half_rows(half)],
                      M[half_rows(half), :, :].rearrange("p k (h m) -> p (k h) m", h=4)[:, :, half_rows(half)],
                      ACT.Copy).then_inc(g["abd_done"], 1)

            act.wait_ge(g["pool_fills"], 5)
            nc.scalar.preload_act_table_set("natural_log_exp_and_others")
            run({"products": products, "ln_square": ln_square, "ln_var": ln_var, "project": project, "scores": scores, "den": den,
                 "den_exp": den_exp, "fc1": fc1, "queries": queries, "blk_scores": blk_scores, "blk_den": blk_den, "wx": wx_})
            act.wait_ge(g["bn_var"], 1)
            A(stat[:, 7:8], stat[:, 6:7], ACT.Ln, bias=eps[:, 0:1]).then_inc(g["bn_log"], 1)
            act.wait_ge(g["bn_log"], 1)
            A(stat[:, 8:9], stat[:, 7:8], ACT.Exp, scale=-0.5).then_inc(g["bn_rstd"], 1)
            nc.scalar.preload_act_table(ACT.Sigmoid)
            def states(step, i):
                return A(ys[:, step, i * BR:(i + 1) * BR, :], rnn_bank(step, i), ACT.Sigmoid)

            order = [(step, i) for first in FIRSTS for step in range(first, L) for i in range(RUNNERS)]
            for n, (step, i) in enumerate(order):
                act.wait_ge(g["pre_mm"], n + 1)
                states(step, i).then_inc(g["y_done"], 1)
            act.wait_ge(g["flag_b"], 1)
            moved = act.value_load(flag[0:1, 0:1])
            with act.If(moved):
                with act.Fori(0, ALL_PASSES) as i:
                    for step in range(L):
                        for runner in range(RUNNERS):
                            act.wait_ge(g["xpre_mm"], i * (L * RUNNERS) + step * RUNNERS + runner + 1)
                            states(step, runner).then_inc(g["xy_done"], 1)

        @block.vector
        def _(dve):
            TT, TS, STT = nc.vector.tensor_tensor, nc.vector.tensor_scalar, nc.vector.scalar_tensor_tensor

            def products():
                dve.wait_ge(g["early_in"], 16)
                dve.wait_ge(g["rest_in"], 16)
                nc.vector.tensor_copy(unit_sel[:], t["unit_select"]).then_inc(g["unit_sel_done"], 1)

            def ln_mean(b, which, i):
                if which == 1 and b == 1:
                    dve.wait_ge(g["x_in"], 32)
                dve.wait_ge(g["ln_mean"], ln_no(b, which, i) + 1)
                TT(ln_bufs(b, which, i)["ln_d"], ln_in(b, which, i), ln_bank(b, which, i, 0), ALU.subtract).then_inc(g["ln_ctr"], 1)

            def ln_scale(b, which, i):
                buf = ln_bufs(b, which, i)
                dve.wait_ge(g["ln_rstd"], ln_no(b, which, i) + 1)
                TT(ln_dst(b, which, i), buf["ln_d"], buf["ln_r"], ALU.mult).then_inc(g["ln_norm"], 1)
                if which < 3:
                    dve.wait_ge(g["ln_norm"], ln_no(b, which, i) + 1)
                    TS(x_ln[:], ln_dst(b, which), v[f"ln{which}_w"], v[f"ln{which}_b"], ALU.mult, ALU.add).then_inc(g["ln_out"], 1)

            def project(b):
                if b:
                    dve.wait_ge(g["qk_lo"], b)
                for q in range(2):
                    dve.wait_ge(g["qk_hi"], 2 * b + q + 1)
                    TT(qk_rest[:, q, :], R[:, q, :], hi_rows[:, q, :], ALU.subtract).then_inc(g["qk_rst"], 1)

            def split(b):
                for q in range(2):
                    dve.wait_ge(g["qk_rst"], 2 * b + q + 1)
                    nc.vector.tensor_copy(mid_rows[:, q, :], qk_rest[:, q, :]).then_inc(g["qk_mid"], 1)
                for q in range(2):
                    dve.wait_ge(g["qk_mid"], 2 * b + q + 1)
                    last = TT(qk_rows[:, 2 + q, :], qk_rest[:, q, :], mid_rows[:, q, :], ALU.subtract)
                last.then_inc(g["qk_lo"], 1)

            def max_piece(b, half, i):
                row, kh = divmod(i, 2)
                n = (2 * b + half) * PIECES + i
                dve.wait_ge(g["max_mm"], n + 1)
                nc.vector.tensor_reduce(part_max[:, row, kh:kh + 1], max_ring(n)[n % len(max_ring(n))], AX_X, ALU.max).then_inc(g["max_red"], 1)

            def max_neg(b, half):
                dve.wait_ge(g["max_red"], (2 * b + half + 1) * PIECES)
                for p in range(PARTS):
                    last = nc.vector.tensor_reduce(neg_max[:, p, :], part_max[:, :, :], AX_X, ALU.max, negate=True)
                last.then_inc(g["negmax"], 1)

            def max_rows(b, half):
                hn = 2 * b + half
                dve.wait_ge(g["negmax_t"], hn + 1)
                nc.vector.tensor_copy(mx_hi[:], M[0:PARTS * ROWS, 0, 0:P]).then_inc(g["mx_h"], 1)
                dve.wait_ge(g["mx_h"], hn + 1)
                STT(mx_rest[:], mx_hi[:], t["part_scale"][0:PARTS * ROWS, 2:3], M[0:PARTS * ROWS, 0, 0:P],
                    ALU.mult, ALU.add).then_inc(g["mx_r"], 1)

            def max_parts(b, half):
                hn = 2 * b + half
                dve.wait_ge(g["mx_r"], hn + 1)
                nc.vector.tensor_copy(mx_mid[:], mx_rest[:]).then_inc(g["mx_m"], 1)
                dve.wait_ge(g["mx_m"], hn + 1)
                if hn:
                    dve.wait_ge(g["shift_in"], 16 * PARTS * hn)
                STT(mx_part[:], mx_mid[:], t["part_scale"][0:PARTS * ROWS, 3:4], mx_rest[:], ALU.mult, ALU.add).then_inc(g["mx_done"], 1)

            def values(b, u):
                half, j = divmod(u, KT)
                if j < KT - 1:
                    return
                dve.wait_ge(g["pv_mm"], b * UNITS + u + 1)
                if b:
                    dve.wait_ge(g["o_normed"], 2 * b)
                nc.vector.tensor_copy(o_sb[:, half, :], O[:]).then_inc(g["o_copied"], 1)

            def o_norm_(b, half):
                if half == 0:
                    dve.wait_ge(g["rden_done"], b + 1)
                n = 2 * b + half + 1
                _, first, step = (x[:, half, :] for x in recip_bufs(b))
                TT(step, pair(b)[:, half, :], first, ALU.mult).then_inc(g["den_prod"], 1)
                dve.wait_ge(g["den_prod"], n)
                STT(step, step, 2.0, first, ALU.subtract, ALU.mult, reverse0=True).then_inc(g["rden_new"], 1)
                dve.wait_ge(g["rden_new"], n)
                TT(o_norm[:, half, :], o_sb[:, half, :], step, ALU.mult).then_inc(g["o_normed"], 1)

            def proj(b):
                dve.wait_ge(g["proj_mm"], b + 1)
                STT(x1[:], single(b), v["proj_b"], X[:, b, :], ALU.add, ALU.add).then_inc(g["x1_done"], 1)

            def fc2(b):
                dve.wait_ge(g["fc2_mm"], b + 1)
                STT(x2s[b % 2][:], single(b), v["fc2_b"], x1[:], ALU.add, ALU.add).then_inc(g["x2_done"], 1)

            def keys(b):
                dve.wait_ge(g["ln_norm"], ln_no(b, 3) + 1)
                if b:
                    dve.wait_ge(g["s1_mm"], STAGES * b)
                nc.vector.tensor_copy(xbd[0:C, PAD:PAD + HALF, 0], xh[0:C, :])
                nc.vector.tensor_copy(xbd[C:P, PAD:PAD + HALF, 1], xh[C:P, :]).then_inc(g["xbd_a"], 1)
                dve.wait_ge(g["shift_mm"], b + 1)
                nc.vector.tensor_copy(xbd[C:P, 0:PAD, 1], R[C:P, 2, 0:PAD]).then_inc(g["xbd_pad"], 1)

            def round_keys(b):
                dve.wait_ge(g["xbd_a"], b + 1)
                dve.wait_ge(g["xbd_pad"], b + 1)
                nc.vector.tensor_copy(xbd16[:], xbd[:].rearrange("p k a -> p a k")).then_inc(g["xbd_cast"], 1)

            def round_query(b, h):
                dve.wait_ge(g["z_copied"], b * H1 + h + 1)
                if b and h == 0:
                    dve.wait_ge(g["fin_mm"], b)
                nc.vector.tensor_copy(z16[:, :, h, :], z[:, :, h, :]).then_inc(g["z_cast"], 1)

            def tokens(b, r):
                n = BLOCKS // TOKS
                dve.wait_ge(g["tok_mm"], b * TOKS + r + 1)
                nc.vector.tensor_copy(x_tok[:, r * n:(r + 1) * n, :],
                                      R[:, (2 + r) % 3, :].rearrange("p (k m) -> p k m", m=P)).then_inc(g["tok_copied"], 1)

            def windows(b, r):
                dve.wait_ge(g["sw_mm"], b * STAGES + r + 1)
                TT(s_win[:, r * UPS * 2:(r + 1) * UPS * 2, :], R[:, r % 3, 0:UPS * 2 * GK].rearrange("p (s k) -> p s k", k=GK),
                   t["window_mask"].rearrange("p (s k) -> p s k", k=GK), ALU.add).then_inc(g["sw_masked"], 1)

            def win_max(b, gs):
                dve.wait_ge(g["sw_masked"], b * STAGES + (gs + 1) * STAGES // GSEL)
                nc.vector.tensor_reduce(neg_m1[:, gs, 0, :], s_win.rearrange("p (g s) k -> p g s k", g=GSEL)[:, gs], AX_X, ALU.max,
                                        negate=True).then_inc(g["sw_max"], 1)
                if gs + 1 < GSEL:
                    return
                dve.wait_ge(g["sw_max"], GSEL * (b + 1))
                nc.vector.tensor_copy(neg_m1[:, :, 1, :], neg_m1[:, :, 0, :])
                nc.vector.tensor_copy(neg_m1[:, :, 2, :], neg_m1[:, :, 0, :]).then_inc(g["m1_rep"], 1)

            rows1 = slice(0, PARTS * 2 * UPG)

            def win_rows(b):
                dve.wait_ge(g["m1_t"], b + 1)
                ps = R[rows1, 2, 0:GSEL * P].rearrange("p (g n) -> p g n", g=GSEL)
                nc.vector.tensor_copy(m1_hi[:], ps).then_inc(g["m1_h"], 1)
                dve.wait_ge(g["m1_h"], b + 1)
                STT(m1_rest[:], m1_hi[:], t["part_scale"][rows1, 0:1], ps, ALU.mult, ALU.add).then_inc(g["m1_r"], 1)

            def win_parts(b):
                dve.wait_ge(g["m1_r"], b + 1)
                nc.vector.tensor_copy(m1_mid[:], m1_rest[:]).then_inc(g["m1_m"], 1)
                dve.wait_ge(g["m1_m"], b + 1)
                STT(m1_part[:], m1_mid[:], t["part_scale"][rows1, 1:2], m1_rest[:], ALU.mult, ALU.add).then_inc(g["m1_done"], 1)

            def blk_mask(b, r):
                dve.wait_ge(g["p1_exp"], b * STAGES + r + 1)
                TT(p1[:, r % 2, :], p1[:, r % 2, :], t["block_mask"], ALU.min).then_inc(g["p1_masked"], 1)

            def blk_out(b, r):
                n = b * STAGES + r
                dve.wait_ge(g["rden1_done"], n + 1)
                dve.wait_ge(g["pv1_mm"], n + 1)
                k = TG // STAGES
                TT(y1[:, :, r * k:(r + 1) * k, :].rearrange("p h t q -> p t h q"),
                   pv1_bank(b, r).rearrange("p (t h q) -> p t h q", h=H1, q=TQ),
                   rden[:, r % 2, :].rearrange("p (t h q) -> p t h q", h=H1, q=TQ), ALU.mult).then_inc(g["y1_done"], 1)

            def wx_part(b, i):
                dve.wait_ge(g["wx_copied"], b + 1 + i)
                nc.vector.bn_stats(bn_parts[:, b + i, :], wx[:, :, b, chunks(b, i)]).then_inc(g["bn_part"], 1)

            def unify(b, h0, i):
                if h0 + 2 < H1:
                    return
                r0, r1 = unify_rounds(b, i)
                dve.wait_ge(g["fin_mm"], b + 1 + i)
                STT(x3[:, b, r0 * RC:r1 * RC], unify_bank(b, i)[:, r0 * RC:r1 * RC], v["attn_b"], x2s[b % 2][:, r0 * RC:r1 * RC],
                    ALU.add, ALU.add).then_inc(g["x3_done"], 1)

            nc.vector.memset(abd[:], 0.0).then_inc(g["fills"], 1)
            nc.vector.memset(gbd[:], 0.0).then_inc(g["fills"], 1)
            dve.wait_ge(g["x0_in"], 32)
            dve.wait_ge(g["first_in"], 16)
            run({"products": products, "ln_mean": ln_mean, "ln_scale": ln_scale, "project": project, "split": split,
                 "o_norm": o_norm_, "round": round_keys, "wx": wx_part, "max_piece": max_piece, "max_neg": max_neg,
                 "max_rows": max_rows, "max_parts": max_parts, "values": values, "proj": proj, "fc2": fc2, "keys": keys,
                 "round_query": round_query, "tokens": tokens, "windows": windows, "win_max": win_max, "win_rows": win_rows, "win_parts": win_parts,
                 "blk_mask": blk_mask, "blk_out": blk_out, "unify": unify})

            dve.wait_ge(g["bn_part"], WX_PARTS)
            nc.vector.bn_aggr(stat[:, 0:2], bn_parts[:]).then_inc(g["bn_own"], 1)
            dve.wait_ge(g["bn_mm"], 1)
            TT(stat[:, 3:4], R[:, 0, 0:1], stat[:, 0:1], ALU.subtract).then_inc(g["bn_shift"], 1)
            TS(stat[:, 5:6], R[:, 0, 0:1], -1.0, None, ALU.mult).then_inc(g["bn_mean"], 1)
            dve.wait_ge(g["bn_shift"], 1)
            TT(stat[:, 4:5], stat[:, 3:4], stat[:, 3:4], ALU.mult).then_inc(g["bn_sq"], 1)
            dve.wait_ge(g["bn_sq"], 1)
            TT(stat[:, 6:7], R[:, 0, 1:2], stat[:, 4:5], ALU.add).then_inc(g["bn_var"], 1)
            dve.wait_ge(g["bn_rstd"], 1)
            TT(stat[:, 9:10], stat[:, 8:9], v["gamma"], ALU.mult).then_inc(g["bn_a"], 1)
            dve.wait_ge(g["bn_a"], 1)
            STT(stat[:, 10:11], stat[:, 5:6], stat[:, 9:10], v["beta"], ALU.mult, ALU.add).then_inc(g["bn_b"], 1)
            dve.wait_ge(g["bn_b"], 1)
            for steps in (wx[:, FIRSTS[0]:, :, :], wx[:, 0:FIRSTS[0], :, :]):
                flat = steps.rearrange("p s b c -> p (s b c)")
                TS(flat, flat, stat[:, 9:10], stat[:, 10:11], ALU.mult, ALU.add).then_inc(g["bn_done"], 1)

            def result(step):
                return TT(res[:].rearrange("p b (c s) -> p b c s", s=L)[:, :, :, step], ys[:, step],
                          x3[:].rearrange("p b (c s) -> p b c s", s=L)[:, :, :, step], ALU.add)

            def new_starts(dst, last_sem):
                nc.vector.tensor_copy(dst[:, :, 1:CH], ys[:, L - 1, :, 0:CH - 1])
                nc.vector.tensor_copy(dst[:, :, 0], R[:, 0, 0:B]).then_inc(last_sem, 1)

            dve.wait_ge(g["gram_mm"], 1)
            nc.vector.tensor_reduce(stat[:, 11:12], R[:, 2, 0:P], AX_X, ALU.add, apply_absolute_value=True).then_inc(g["gram_sum"], 1)
            dve.wait_ge(g["gram_sum"], 1)
            TS(stat[:, 14:15], stat[:, 11:12], 1.0 / GRAM_LIMIT, None, ALU.mult).then_inc(g["gram_share"], 1)
            for ps in range(1, len(FIRSTS)):
                dve.wait_ge(g["ends_mm"], ps)
                new_starts(y0, g["y0_done"])
            for step in range(L):
                dve.wait_ge(g["y_done"], (WARM + step + 1) * RUNNERS)
                last = result(step)
            last.then_inc(g["res_done"], 1)
            dve.wait_ge(g["ends_mm"], len(FIRSTS))
            new_starts(y0n, g["y0_moved"])
            dve.wait_ge(g["y0_moved"], 1)
            TT(ydiff[:], y0n[:], y0[:], ALU.subtract).then_inc(g["ydiff_a"], 1)
            dve.wait_ge(g["ydiff_a"], 1)
            nc.vector.tensor_reduce(stat[:, 15:16], ydiff[:].rearrange("p b c -> p (b c)"), AX_X, ALU.max,
                                    apply_absolute_value=True).then_inc(g["ydiff_m"], 1)
            dve.wait_ge(g["ydiff_m"], 1)
            STT(stat[:, 12:13], stat[:, 15:16], 1.0 / START_TOL, stat[:, 14:15], ALU.mult, ALU.max).then_inc(g["ydiff_b"], 1)
            dve.wait_ge(g["dmax_t"], 1)
            nc.vector.tensor_reduce(stat[0:1, 13:14], R[0:1, 1, 0:P], AX_X, ALU.max).then_inc(g["flag_a"], 1)
            dve.wait_ge(g["flag_a"], 1)
            TS(flag[0:1, 0:1], stat[0:1, 13:14], 1.0, None, ALU.is_gt)
            nc.vector.tensor_copy(y0[:], y0n[:]).then_inc(g["flag_b"], 1)
            dve.wait_ge(g["flag_b"], 1)
            moved = dve.value_load(flag[0:1, 0:1])
            with dve.If(moved):
                with dve.Fori(0, ALL_PASSES) as i:
                    dve.wait_ge(g["xends_mm"], i + 1)
                    new_starts(y0, g["xy0_done"])
                dve.wait_ge(g["out_done"], 32)
                for step in range(L):
                    last = result(step)
                last.then_inc(g["xres_done"], 1)


def kernel(**inputs):
    import numpy as np
    import concourse.bacc as bacc
    from concourse.bass_utils import run_bass_kernel_spmd

    f = np.float32
    g = {k: np.asarray(x) for k, x in inputs.items()}

    def both(m):
        o = np.zeros((2 * m.shape[0], 2 * m.shape[1]), m.dtype)
        o[:m.shape[0], :m.shape[1]] = m
        o[m.shape[0]:, m.shape[1]:] = m
        return o

    def twice(x):
        return np.concatenate([x, x])

    pp = np.arange(P)
    arr = {"ident": np.eye(P, dtype=f)}
    arr["mean_c"] = both(np.full((C, C), 1.0 / C, f))
    arr["mean_all"] = (pp[:, None] % C == pp[None] % C).astype(f) / f(2)
    arr["shift_half"] = (pp[:, None] + C == pp[None]).astype(f)
    arr["den_select"] = (pp[:, None] == pp[None] // HP * HP + HD).astype(f)
    q, k = (pp % (H1 * TQ)) % TQ, np.arange(GK)
    ok = (k[None] >= q[:, None]) & (k[None] - q[:, None] < W)
    arr["window_mask"] = np.tile(np.where(ok, 0.0, -1e30).astype(f), (1, 2 * UPS))
    col = np.arange(BQ)
    q = col // (H1 * TQ) * TQ + col % TQ
    ok = (pp[:, None] // 2 >= q[None]) & (pp[:, None] // 2 - q[None] < W)
    arr["block_mask"] = np.tile(np.where(ok, 1e30, 0.0).astype(f), (1, BPS))
    row = np.arange(PARTS * 2 * UPG)
    unit, half = row % (2 * UPG) // 2, row % 2
    arr["unit_select"] = ((unit[:, None, None] == np.arange(UPG)[None, :, None])
                          & (half[:, None, None] == (pp % 2)[None, None])).astype(f)
    arr["block_ones"] = (pp[:, None] % 2 == pp[None] // C).astype(f)
    arr["part_scale"] = np.stack([-(pp >= r).astype(f) for r in (2 * UPG, 4 * UPG, ROWS, 2 * ROWS)], 1)

    arr["x"] = np.ascontiguousarray(g["x"].reshape(B, C, N))
    wqkv = g["L0_conv_qkv_w"]
    turned = [wqkv[i * C:(i + 1) * C].reshape(H0, HD, C).transpose(1, 0, 2).reshape(C, C) for i in range(2)]
    arr["wq"], arr["wk"], arr["wv"] = both(turned[0].T), both(turned[1].T), both(wqkv[2 * C:].T)
    wp = np.zeros((P, C), f)
    for h in range(H0):
        wp[h * HP:h * HP + HD] = g["L0_conv_proj_w"].T[h * HD:(h + 1) * HD]
    arr["wproj"] = wp
    w1 = np.zeros((P, 2, P), f)
    for half in range(2):
        w1[half * C:(half + 1) * C, half] = g["L0_conv_fc1_w"].T
    arr["wfc1"] = w1
    arr["wfc2"] = np.ascontiguousarray(g["L0_conv_fc2_w"].T)

    def padded(m):
        return np.concatenate([m, np.zeros_like(m)])
    for n, w in (("w1q", "L1_attn_Wq"), ("w1k", "L1_attn_Wk"), ("w1v", "L1_attn_Wv")):
        arr[n] = padded(np.ascontiguousarray(g[w].reshape(H1, C, C).transpose(1, 0, 2)))
    arr["w1u"] = padded(np.ascontiguousarray(g["L1_attn_Wu"].T.reshape(H1, C, C).transpose(1, 0, 2)))
    arr["w_in"] = both(g["L1_ffn_W"].T)
    arr["v_rec"] = both(g["L1_ffn_V"].T)
    vecs = {"ln1_w": "L0_conv_ln1_w", "ln1_b": "L0_conv_ln1_b", "proj_b": "L0_conv_proj_b", "ln2_w": "L0_conv_ln2_w",
            "ln2_b": "L0_conv_ln2_b", "fc2_b": "L0_conv_fc2_b", "attn_b": "L1_attn_bu", "gamma": "L1_ffn_gamma",
            "beta": "L1_ffn_beta"}
    arr["vectors"] = np.stack([g["L0_conv_fc1_b"] if n == "fc1_b" else twice(g[vecs[n]]) for n in VECTORS], 1)

    nc = bacc.Bacc("TRN2", target_bir_lowering=False, num_devices=1)
    arrays, aps = {"x": arr["x"]}, {}
    for which, cols in (("first", FIRST), ("rest", REST), ("early", EARLY)):
        arrays[which] = np.zeros((P, sum(cols.values())), f)
        at = 0
        for n, width in cols.items():
            arrays[which][:arr[n].shape[0], at:at + width] = arr[n].reshape(arr[n].shape[0], width)
            at += width
    for n in arrays:
        aps[n] = nc.dram_tensor(n, arrays[n].shape, mybir.dt.from_np(arrays[n].dtype), kind="ExternalInput").ap()
    out = nc.dram_tensor("result", (B, C, N), F32, kind="ExternalOutput").ap()
    build(nc, aps, out)
    r = run_bass_kernel_spmd(nc, [arrays], core_ids=[0])
    return r.results[0]["result"].reshape(B, C, 32, 32)
```
